# Optimizing a Trainium2 kernel written in Bass

```python
import numpy as np
import jax
import jax.numpy as jnp

def _softmax(x, axis=-1):
    return jax.nn.softmax(x, axis=axis)

def _gelu(x):
    return jax.nn.gelu(x, approximate=True)

def _silu(x):
    return jax.nn.silu(x)

def _sigmoid(x):
    return jax.nn.sigmoid(x)

def _layernorm(x, axis=-1, eps=1e-05):
    m = jnp.mean(x, axis=axis, keepdims=True)
    v = jnp.var(x, axis=axis, keepdims=True)
    return (x - m) / jnp.sqrt(v + eps)

def _scatter_add(tgt, idx, src, axis=0):
    return tgt.at[idx].add(src)

def _segment_sum(src, seg, n):
    return jax.ops.segment_sum(src, seg, n)
kernel_name = 'mk_seq_postln_d1_jaxref_r8_66d5f3'

def setup_inputs(seed: int=0):
    np.random.seed(seed)
    _w = jnp.asarray

    def _L0_attn_setup():
        import jax, jax.numpy as jnp
        import numpy as np
        D_MODEL = 128
        D_INNER = 256
        D_STATE = 16
        D_CONV = 4
        DT_RANK = 64
        B_SZ = 2
        L_SEQ = 256
        EPS = 1e-06

        def _silu(v):
            return v * jax.nn.sigmoid(v)
        key = jax.random.key(seed)
        ks = jax.random.split(key, 9)

        def g(k, shape, scale=0.02):
            return jax.random.normal(k, shape, jnp.float32) * scale
        return {'x': jax.random.normal(ks[0], (B_SZ, L_SEQ, D_MODEL), jnp.float32), 'ln_gamma': jnp.ones((D_MODEL,), jnp.float32), 'ln_beta': jnp.zeros((D_MODEL,), jnp.float32), 'in_proj_w': g(ks[1], (2 * D_INNER, D_MODEL)), 'conv_w': g(ks[2], (D_INNER, 1, D_CONV), 0.1), 'conv_b': g(ks[3], (D_INNER,), 0.1), 'x_proj_w': g(ks[4], (DT_RANK + 2 * D_STATE, D_INNER)), 'dt_proj_w': g(ks[5], (D_INNER, DT_RANK), 0.1), 'dt_proj_b': g(ks[6], (D_INNER,), 0.1), 'A_log': jnp.log(jnp.broadcast_to(jnp.arange(1, D_STATE + 1, dtype=jnp.float32), (D_INNER, D_STATE))), 'D': jnp.ones((D_INNER,), jnp.float32), 'out_proj_w': g(ks[7], (D_MODEL, D_INNER))}
    _L0_attn_in = _L0_attn_setup()

    def _L0_ffn_setup():
        import jax, jax.numpy as jnp
        import numpy as np
        D = 128
        H = 512
        E = 8
        K = 2
        B, S = (4, 256)
        key = jax.random.key(seed)
        ks = jax.random.split(key, 8)

        def lin(k, fan_in, shape):
            bound = 1.0 / np.sqrt(fan_in)
            return jax.random.uniform(k, shape, jnp.float32, -bound, bound)
        return {'x': jax.random.normal(ks[0], (B, S, D), jnp.float32), 'Wg': lin(ks[1], D, (D, E)), 'bg': lin(ks[2], D, (E,)), 'W1': lin(ks[3], D, (E, D, H)), 'b1': lin(ks[4], D, (E, H)), 'W2': lin(ks[5], H, (E, H, D)), 'b2': lin(ks[6], H, (E, D))}
    _L0_ffn_in = _L0_ffn_setup()
    _d = {'L0_attn_x': _L0_attn_in['x'], 'L0_attn_ln_gamma': _L0_attn_in['ln_gamma'], 'L0_attn_ln_beta': _L0_attn_in['ln_beta'], 'L0_attn_in_proj_w': _L0_attn_in['in_proj_w'], 'L0_attn_conv_w': _L0_attn_in['conv_w'], 'L0_attn_conv_b': _L0_attn_in['conv_b'], 'L0_attn_x_proj_w': _L0_attn_in['x_proj_w'], 'L0_attn_dt_proj_w': _L0_attn_in['dt_proj_w'], 'L0_attn_dt_proj_b': _L0_attn_in['dt_proj_b'], 'L0_attn_A_log': _L0_attn_in['A_log'], 'L0_attn_D': _L0_attn_in['D'], 'L0_attn_out_proj_w': _L0_attn_in['out_proj_w'], 'L0_ffn_Wg': _L0_ffn_in['Wg'], 'L0_ffn_bg': _L0_ffn_in['bg'], 'L0_ffn_W1': _L0_ffn_in['W1'], 'L0_ffn_b1': _L0_ffn_in['b1'], 'L0_ffn_W2': _L0_ffn_in['W2'], 'L0_ffn_b2': _L0_ffn_in['b2']}
    _x0 = _d['L0_attn_x']
    _d['L0_attn_x'] = jax.random.normal(jax.random.fold_in(jax.random.key(seed), 1), (2, 2048, 128), dtype=_x0.dtype)
    del _x0
    return _d

def reference(L0_attn_x, L0_attn_ln_gamma, L0_attn_ln_beta, L0_attn_in_proj_w, L0_attn_conv_w, L0_attn_conv_b, L0_attn_x_proj_w, L0_attn_dt_proj_w, L0_attn_dt_proj_b, L0_attn_A_log, L0_attn_D, L0_attn_out_proj_w, L0_ffn_Wg, L0_ffn_bg, L0_ffn_W1, L0_ffn_b1, L0_ffn_W2, L0_ffn_b2):

    def _L0_attn_ref(x, ln_gamma, ln_beta, in_proj_w, conv_w, conv_b, x_proj_w, dt_proj_w, dt_proj_b, A_log, D, out_proj_w):
        import jax, jax.numpy as jnp
        import numpy as np
        D_MODEL = 128
        D_INNER = 256
        D_STATE = 16
        D_CONV = 4
        DT_RANK = 64
        B_SZ = 2
        L_SEQ = 256
        EPS = 1e-06

        def _silu(v):
            return v * jax.nn.sigmoid(v)
        B, L, _ = x.shape
        mu = x.mean(-1, keepdims=True)
        var = x.var(-1, keepdims=True)
        h = (x - mu) / jnp.sqrt(var + EPS) * ln_gamma + ln_beta
        xz = jnp.einsum('bld,ed->bel', h, in_proj_w)
        u, z = jnp.split(xz, 2, axis=1)
        up = jnp.pad(u, ((0, 0), (0, 0), (D_CONV - 1, 0)))
        uc = jax.lax.conv_general_dilated(up, conv_w, (1,), 'VALID', dimension_numbers=('NCH', 'OIH', 'NCH'), feature_group_count=D_INNER)
        uc = _silu(uc + conv_b[None, :, None])
        x_dbl = jnp.einsum('bdl,ed->ble', uc, x_proj_w)
        dt, Bm, Cm = jnp.split(x_dbl, [DT_RANK, DT_RANK + D_STATE], axis=-1)
        delta = jnp.einsum('blr,dr->bdl', dt, dt_proj_w) + dt_proj_b[None, :, None]
        delta = jax.nn.softplus(delta)
        A = -jnp.exp(A_log)
        deltaA = jnp.exp(jnp.einsum('bdl,dn->bdln', delta, A))
        Bm = jnp.transpose(Bm, (0, 2, 1))
        Cm = jnp.transpose(Cm, (0, 2, 1))
        deltaB_u = jnp.einsum('bdl,bnl,bdl->bdln', delta, Bm, uc)

        def step(state, inp):
            dA, dBu, Ct = inp
            state = dA * state + dBu
            y = jnp.einsum('bdn,bn->bd', state, Ct)
            return (state, y)
        init = jnp.zeros((B, D_INNER, D_STATE), jnp.float32)
        _, ys = jax.lax.scan(step, init, (jnp.moveaxis(deltaA, 2, 0), jnp.moveaxis(deltaB_u, 2, 0), jnp.moveaxis(Cm, 2, 0)))
        y = jnp.moveaxis(ys, 0, 2)
        y = y + uc * D[None, :, None]
        y = y * _silu(z)
        out = jnp.einsum('bdl,ed->ble', y, out_proj_w)
        return out + x

    def _L0_ffn_ref(x, Wg, bg, W1, b1, W2, b2):
        import jax, jax.numpy as jnp
        import numpy as np
        D = 128
        H = 512
        E = 8
        K = 2
        B, S = (4, 256)
        B_, S_, D_ = x.shape
        xt = x.reshape(-1, D_)
        logits = xt @ Wg + bg
        scores = jax.nn.softmax(logits, axis=-1)
        topk_probs, topk_idx = jax.lax.top_k(scores, K)
        h = jnp.einsum('nd,edh->enh', xt, W1) + b1[:, None, :]
        h = jax.nn.gelu(h, approximate=False)
        eo = jnp.einsum('enh,ehd->end', h, W2) + b2[:, None, :]
        eo = jnp.transpose(eo, (1, 0, 2))
        sel = jnp.take_along_axis(eo, topk_idx[:, :, None], axis=1)
        out = jnp.einsum('nk,nkd->nd', topk_probs, sel)
        return out.reshape(B_, S_, D_)
    x = L0_attn_x
    x = _layernorm(x + _L0_attn_ref(x, L0_attn_ln_gamma, L0_attn_ln_beta, L0_attn_in_proj_w, L0_attn_conv_w, L0_attn_conv_b, L0_attn_x_proj_w, L0_attn_dt_proj_w, L0_attn_dt_proj_b, L0_attn_A_log, L0_attn_D, L0_attn_out_proj_w), axis=-1)
    x = _layernorm(x + _L0_ffn_ref(x, L0_ffn_Wg, L0_ffn_bg, L0_ffn_W1, L0_ffn_b1, L0_ffn_W2, L0_ffn_b2), axis=-1)
    return x

_drawn_inputs = setup_inputs


def setup_inputs(seed=0):
    import zlib

    import numpy as np

    out = dict(_drawn_inputs(seed))
    spreads = {'L0_attn_ln_gamma': (1.0, 0.6), 'L0_attn_ln_beta': (0.0, 0.8), 'L0_attn_D': (1.0, 0.6)}
    factors = {'L0_attn_in_proj_w': 8.0,
     'L0_attn_conv_w': 8.0,
     'L0_attn_conv_b': 8.0,
     'L0_attn_x_proj_w': 8.0,
     'L0_attn_dt_proj_w': 8.0,
     'L0_attn_dt_proj_b': 8.0,
     'L0_attn_A_log': 8.0,
     'L0_attn_out_proj_w': 8.0,
     'L0_ffn_bg': 4.295,
     'L0_ffn_b1': 8.0,
     'L0_ffn_b2': 6.759}
    for name, (base, spread) in spreads.items():
        noise = np.random.default_rng([zlib.crc32(name.encode()), seed]).standard_normal(out[name].shape)
        drawn = base * np.exp(spread * noise) if base else spread * noise
        out[name] = jnp.asarray(drawn.astype(out[name].dtype))
    for name, factor in factors.items():
        out[name] = (out[name] * factor).astype(out[name].dtype)
    return out
```

```python
from contextlib import ExitStack

import concourse.bass as bass
from concourse import mybir

ALU = mybir.AluOpType
ACT = mybir.ActivationFunctionType
BF16 = mybir.dt.bfloat16
F32 = mybir.dt.float32
U32 = mybir.dt.uint32
AX_X = mybir.AxisListType.X

P = 128
B, L, D = 2, 2048, 128
DI, N, RANK, TAPS = 256, 16, 64, 4
E, H = 8, 512
T = 512
UNITS = B * L // T
TT = T // P
HALVES = DI // P
CH = P // N
QUADS = 8
HK = H // P
NTOK = B * L
MAXT = 2 * NTOK // P + E
LIST = E * NTOK + E * P
LC = LIST // P
ROWS = 2 * NTOK + 2 * E * P


class Unit:

    def __init__(self, i, k):
        self.i, self.k, self.b = i, k, k % 2

    def value(self, per_unit, plus):
        fixed = per_unit * self.k + plus
        if self.i is None:
            return fixed
        assert fixed > 0
        return self.i * (2 * per_unit) + fixed

    def chunk(self, plus=0):
        c = self.k // 2 + plus
        return c if self.i is None else self.i + c

    def next(self):
        return Unit(self.i, self.k + 1)

    def prev(self):
        return Unit(self.i, self.k - 1)


class Tile:

    def __init__(self, i, k):
        self.i, self.k, self.ring = i, k, k % 4

    def value(self, plus, scale=1):
        fixed = scale * (self.k + plus)
        if self.i is None:
            return fixed
        assert fixed > 0
        return self.i * (4 * scale) + fixed

    def dmas(self, plus):
        fixed = 16 * (self.k // 4 + plus)
        return fixed if self.i is None else self.i * 16 + fixed

    def at(self, size=1):
        fixed = self.k * size
        return bass.ds(fixed if self.i is None else self.i * (4 * size) + fixed, size)

    def back(self, lag):
        return Tile(self.i, self.k - lag)


def mamba_moe(nc, consts, spare_rows, spill, row_list, results, x, ln_gamma, ln_beta, in_proj_w, conv_w, conv_b, x_proj_w, dt_proj_w, dt_proj_b,
              A_log, Dskip, out_proj_w, Wg, bg, W1, b1, W2, b2, out):
    with ExitStack() as ctx:
        def sb(name, shape, dt=F32):
            return ctx.enter_context(nc.sbuf_tensor(name, shape, dt))

        def sem(name):
            return ctx.enter_context(nc.semaphore(name))

        def after(eng, semaphore, value):
            if isinstance(value, int) and value <= 0:
                return
            eng.wait_ge(semaphore, value)

        ident = sb("ident", [P, P])
        sel = sb("sel", [96, 4, P], BF16)
        fold = sb("fold", [P, 160])
        wtapT = sb("wtapT", [P, HALVES, TAPS, P])
        wzT = sb("wzT", [P, HALVES, P])
        woutT = sb("woutT", [P, HALVES, D])
        wxpT = sb("wxpT", [P, HALVES, RANK + 2 * N])
        wdtT = sb("wdtT", [RANK, HALVES, P])
        negA = sb("negA", [P, DI * N // P])
        aexp = sb("aexp", [P, DI * N // P])
        gam = sb("gam", [P, 1])
        bet = sb("bet", [P, 1])
        cw = sb("cw", [P, HALVES, TAPS])
        cb = sb("cb", [P, HALVES])
        dtb = sb("dtb", [P, HALVES])
        dsk = sb("dsk", [P, HALVES])
        wg_sb = sb("wg_sb", [P, E])
        bg_rep = sb("bg_rep", [P, E])
        before = sb("before", [P, P], BF16)
        ones = sb("ones", [P, P], BF16)
        w1_sb = sb("w1_sb", [P, E, H])
        w2_sb = sb("w2_sb", [P, E, HK, D])
        minus_half = sb("minus_half", [P, TT])
        kc = sb("kc", [P, CONSTS])
        _, _, base, thresholds, numbers, rows_of, lane, one8 = [
            kc[:, a:b] for a, b in zip(K_AT[:-1], K_AT[1:])]
        zero1 = sb("zero1", [P, 1])
        zero2 = sb("zero2", [P, 1])

        xin = [sb(f"xin{b}", [P, TT, D]) for b in range(B)]
        hT = [sb(f"hT{b}", [P, T + TAPS - 1]) for b in range(B)]
        uc = [sb(f"uc{b}", [P, HALVES, T]) for b in range(B)]
        sz = [sb(f"sz{b}", [P, HALVES, T]) for b in range(B)]
        Brep = [sb(f"Brep{b}", [P, T]) for b in range(B)]
        Crep = [sb(f"Crep{b}", [P, T]) for b in range(B)]
        dparts = [sb(f"dparts{b}", [96, HALVES * 4, T], BF16) for b in range(B)]
        uparts = [sb(f"uparts{b}", [96, HALVES * 4, T], BF16) for b in range(B)]
        state = sb("state", [P, B, HALVES, 4, 4])
        bst = sb("bst", [P, TT, 6])
        mv = sb("mv", [P, TT, 2])
        veps = sb("veps", [P, TT])
        rstd = sb("rstd", [P, TT])
        xdbl = sb("xdbl", [RANK + 2 * N, T])
        pre = sb("pre", [P, 4, T])
        t1, t2 = pre[:, 0:2, :], pre[:, 2:4, :]
        t3 = sb("t3", [P, HALVES, T])
        xhat = sb("xhat", [P, TT, D])
        t4 = sb("t4", [P, HALVES, T])
        dpart = [sb(f"dpart{p}", [P, HALVES, T], BF16) for p in range(3)]
        upart = [sb(f"upart{p}", [P, HALVES, T], BF16) for p in range(3)]
        decay = sb("decay", [P, 4, T])
        inflow = sb("inflow", [P, 2, T])
        hs = sb("hs", [P, 2, 4, T])
        hc = sb("hc", [P, 2, 4, T])
        scratch = hs[:].rearrange("p a j t -> p (a j t)")
        win_raw = scratch[:, 0:512].rearrange("p (c d) -> p c d", c=4)
        wtap_raw = scratch[:, 512:1536].rearrange("p (h k d) -> p h k d", h=HALVES, k=TAPS)
        wxp_raw = scratch[0:RANK + 2 * N, 1536:1792]
        wdt_raw = scratch[:, 1792:1920].rearrange("p (h r) -> p h r", h=HALVES)
        wout_raw = scratch[:, 1920:2176]
        alog_raw = scratch[0:DI * N // P, 2176:2304]
        yg = sb("yg", [P, HALVES, T])
        xres = sb("xres", [P, TT, D])
        res = sb("res", [P, TT, D])
        cst = sb("cst", [P, TT, 6])
        cmv = sb("cmv", [P, TT, 2])
        cveps = sb("cveps", [P, TT])
        crstd = sb("crstd", [P, TT])
        xn = sb("xn", [P, TT, D])
        xnT = sb("xnT", [P, T])
        lg = sb("lg", [P, TT, E])
        carrier = sb("carrier", [P, 10])
        top = sb("top", [P, TT, 8])
        topi = sb("topi", [P, TT, 8], U32)
        topf = sb("topf", [P, TT, 2])
        oh = sb("oh", [P, TT, 2, E])
        taken = sb("taken", [P, TT, E], BF16)
        ex = sb("ex", [P, TT, E])
        esum = sb("esum", [P, TT])
        erec = sb("erec", [P, TT])
        probs = sb("probs", [P, UNITS * TT * 2])
        rank = sb("rank", [P, TT, E])
        masked = sb("masked", [P, TT, 2, E])
        run = sb("run", [P, E])
        posf = sb("posf", [P, TT, 2])
        ids = [sb(f"ids{b}", [P, TT, 2]) for b in range(B)]
        pos = [sb(f"pos{b}", [P, TT * 2], U32) for b in range(B)]
        count = sb("count", [P, E])
        plan_room = decay[:].rearrange("p a t -> p (a t)")
        over = plan_room[:, 0:E * NTOK // P].rearrange("p (e n) -> p e n", e=E)
        tiles = sb("tiles", [P, E])
        cum = sb("cum", [P, E])
        past = plan_room[:, 256:256 + MAXT * E].rearrange("p (j e) -> p j e", e=E)
        pastc = plan_room[:, 1024:1024 + MAXT * E].rearrange("p (j e) -> p j e", e=E)
        region = sb("region", [P, MAXT])
        start = sb("start", [P, MAXT])
        expert = sb("expert", [P, MAXT])
        etab = sb("etab", [P, MAXT], U32)
        within = sb("within", [P, MAXT])
        lrow = sb("lrow", [P, MAXT])
        pick = sb("pick", [P, 3, MAXT])
        lists = sb("lists", [P, 3, P])
        dstf = sb("dstf", [P, MAXT])
        srcf = sb("srcf", [P, MAXT])
        fix1 = sb("fix1", [P, MAXT])
        fix2 = sb("fix2", [P, MAXT])
        dst_tab = sb("dst_tab", [P, MAXT], U32)
        src_tab = sb("src_tab", [P, MAXT], U32)
        src_now = sb("src_now", [P, 4], U32)
        dst_now = sb("dst_now", [P, 4], U32)
        b1_rep = hs[:].rearrange("p a j t -> p (a j t)")
        free = hc[:].rearrange("p a j t -> p (a j t)")
        b2_rep = free[:, 0:1024]
        hbuf = free[:, 1024:2048].rearrange("p (a h) -> p a h", a=2)
        hTs = free[:, 2048:3072].rearrange("p (a h) -> p a h", a=2)
        xg = free[:, 3072:3584].rearrange("p (a d) -> p a d", a=4)
        xTs = free[:, 3584:3840].rearrange("p (a d) -> p a d", a=2)
        ybuf = sb("ybuf", [P, 4, D])
        ycomb = decay[:].rearrange("p (b k) (t d) -> p b k t d", b=2, t=TT)
        xcomb = pre[:, 0:2, :].rearrange("p b (t d) -> p b t d", t=TT)
        total = t3[:].rearrange("p b (t d) -> p b t d", t=TT)
        final = t4[:].rearrange("p b (t d) -> p b t d", t=TT)
        pcur = sb("pcur", [P, 2, TT, 2])
        fst = sb("fst", [P, TT, 6])
        fmv = sb("fmv", [P, TT, 2])
        fveps = sb("fveps", [P, TT])
        frstd = sb("frstd", [P, TT])

        bank = [ctx.enter_context(nc.psum_tensor(f"bank{i}", [P, 512], F32)) for i in range(8)]
        drep, urep, ybank, fbanks, mbank = bank[0:2], bank[2:4], bank[4], bank[5:7], bank[7]
        xT_banks, h_banks, hT_banks, o_banks = (bank[0], bank[7]), bank[1:3], bank[3:5], bank[5:7]

        s_w = sem("weights_loaded")
        s_w2 = sem("expert_weights_loaded")
        s_k = sem("pool_constants")
        s_tap = sem("taps_scaled")
        s_pT = sem("weights_transposed")
        s_pe = sem("weights_evacuated")
        s_negA = sem("negA_done")
        s_zero = sem("dve_constants")
        s_x = [sem(f"x_loaded{b}") for b in range(B)]
        s_parts = [sem(f"parts_loaded{b}") for b in range(B)]
        s_rep = [sem(f"bc_loaded{b}") for b in range(B)]
        s_xr = sem("xres_loaded")
        s_sp = sem("sync_steps")
        s_out = sem("out_stored")
        s_spill = sem("xn_spilled")
        s_list = sem("list_filled_with_spare_rows")
        s_zres = sem("results_zeroed")
        s_pos = sem("list_places")
        s_scat = [sem(f"rows_listed{b}") for b in range(B)]
        s_plan = sem("plan_steps")
        s_lists = sem("lists_loaded")
        s_pick = sem("rows_picked")
        s_bias = sem("biases_loaded")
        e_si = sem("source_index")
        e_cg = sem("gather_carrier")
        e_cs = sem("scatter_carrier")
        e_g = [sem(f"rows_gathered{r}") for r in range(4)]
        e_xT = sem("x_transposed")
        e_xe = sem("x_evacuated")
        e_h = sem("hidden_product")
        e_hb = sem("hidden_biased")
        e_hT = sem("hidden_transposed")
        e_ge = sem("gelu_done")
        e_o = sem("output_product")
        e_ob = sem("output_biased")
        e_di = sem("destination_index")
        e_sc = [sem(f"results_scattered{r}") for r in range(4)]
        c_in = [sem(f"sum_operands_loaded{b}") for b in range(2)]
        c_p = sem("probs_copied")
        c_1 = sem("first_added")
        c_2 = sem("second_added")
        s_fst = sem("front_stats")
        s_fag = sem("front_aggr")
        s_fve = sem("front_veps")
        s_frs = sem("front_rstd")
        s_xh = sem("xhat_done")
        s_ff = sem("front_bank_filled")
        s_fd = sem("front_bank_drained")
        s_carry = sem("conv_carry")
        s_silu = sem("silu_done")
        s_abs = sem("abs_relu_done")
        s_e = sem("e_done")
        s_1pe = sem("one_plus_e")
        s_ln = sem("ln_done")
        s_nc = sem("minus_correction")
        s_l1p = sem("log1p_done")
        s_delta = sem("delta_done")
        s_du = sem("du_done")
        s_hi = sem("hi_parts")
        s_r1 = sem("rest1")
        s_mid = sem("mid_parts")
        s_lo = sem("lo_part_du")
        s_lod = sem("lo_part_delta")
        s_dr = sem("delta_rep_filled")
        s_ur = sem("du_rep_filled")
        s_ex = sem("decay_done")
        s_bu = sem("inflow_done")
        s_sc = sem("scan_done")
        s_st = sem("state_kept")
        s_hc = sem("hc_done")
        s_y = sem("y_added")
        s_yd = sem("y_skip_added")
        s_yg = sem("y_gated")
        s_mf = sem("m_bank_filled")
        s_md = sem("m_bank_drained")
        s_res = sem("residual_done")
        s_cst = sem("ln1_stats")
        s_cag = sem("ln1_aggr")
        s_cve = sem("ln1_veps")
        s_crs = sem("ln1_rstd")
        s_xn = sem("xn_done")
        s_gate = sem("gate_steps")
        s_oh = sem("one_hots_done")
        s_gex = sem("gate_exp")
        s_fs2 = sem("ln2_stats")
        s_fa2 = sem("ln2_aggr")
        s_fv2 = sem("ln2_veps")
        s_fr2 = sem("ln2_rstd")
        s_fin = sem("fin_done")

        GATE = 13
        PLAN = 18
        MUSES = ["oproj", "xnT", "logits", "rank"]

        def tile_of(q, j):
            return 16 * (q // 4) + 4 * j + q % 4

        AHEAD = 12

        def tile_steps(eng, step):
            for n in range(AHEAD):
                step(Tile(None, n), lambda lag, n=n: n >= lag)
            with eng.Fori(0, (MAXT - AHEAD) // 4) as i:
                for k in range(4):
                    step(Tile(i, AHEAD + k), lambda lag: True)
            for n in range(MAXT, MAXT + 7):
                step(Tile(None, n), lambda lag, n=n: n - lag < MAXT)

        block = ctx.enter_context(nc.Block())

        @block.sync
        def _(sp):
            def passed(semaphore, value):
                after(sp, semaphore, value)
                sp.sem_inc(s_sp, 1)

            def load_x(u):
                passed(s_xh, u.value(1, -1))
                sp.dma_start(xin[u.b][:], x[u.b, bass.ds(u.chunk() * T, T), :].rearrange("(t p) d -> p t d", p=P))\
                    .then_inc(s_x[u.b], 16)

            def load_xres(u):
                passed(s_res, u.value(1, 0))
                sp.dma_start(xres[:], x[u.b, bass.ds(u.chunk() * T, T), :].rearrange("(t p) d -> p t d", p=P))\
                    .then_inc(s_xr, 16)

            def replicate_bc(u):
                passed(s_fd, u.value(8, 6))
                after(sp, s_hc, u.value(8, -8))
                for i in range(CH):
                    sp.dma_start(Brep[u.b][N * i:N * i + N, :], xdbl[RANK:RANK + N, :]).then_inc(s_rep[u.b], 16)
                    sp.dma_start(Crep[u.b][N * i:N * i + N, :], xdbl[RANK + N:, :]).then_inc(s_rep[u.b], 16)

            def stack_part(u, ready, n, part, dst, p):
                sp.wait_ge(ready, u.value(2, n + 1))
                for j in range(4):
                    sp.dma_start(dst[u.b][32 * p:32 * p + 32, j:j + 5:4, :],
                                 part[p][32 * j:32 * j + 32, :, :]).then_inc(s_parts[u.b], 16)

            def stack_parts(u):
                stack_part(u, s_hi, 0, dpart, dparts, 0)
                stack_part(u, s_hi, 1, upart, uparts, 0)
                stack_part(u, s_mid, 0, dpart, dparts, 1)
                stack_part(u, s_mid, 1, upart, uparts, 1)
                stack_part(u, s_lo, 1, upart, uparts, 2)
                stack_part(u, s_lod, 0, dpart, dparts, 2)

            def spill_xn(u):
                passed(s_xn, u.value(1, 1))
                row = T * u.k if u.i is None else u.i * (2 * T) + T * u.k
                sp.dma_start(spill[bass.ds(row, T), :].rearrange("(t p) d -> p t d", p=P),
                             xn[:]).then_inc(s_spill, 16)

            first, last = Unit(None, 0), Unit(None, UNITS - 1)
            sp.dma_start(xin[0][:], x[0, 0:T, :].rearrange("(t p) d -> p t d", p=P)).then_inc(s_x[0], 16)
            few = nc.allow_non_contiguous_dma(reason="a few hundred elements")
            few.__enter__()
            sp.dma_start(win_raw, in_proj_w.rearrange("(c p) d -> p c d", p=P)).then_inc(s_w, 16)
            sp.dma_start(cw[:], conv_w.rearrange("(h p) a k -> p h (a k)", p=P)).then_inc(s_w, 16)
            sp.dma_start(wxp_raw, x_proj_w).then_inc(s_w, 16)
            sp.dma_start(wdt_raw, dt_proj_w.rearrange("(h p) r -> p h r", p=P)).then_inc(s_w, 16)
            sp.dma_start(wout_raw, out_proj_w).then_inc(s_w, 16)
            sp.dma_start(alog_raw, A_log.rearrange("(g i) n -> g (i n)", i=CH)).then_inc(s_w, 16)
            for dst, src in ((gam, ln_gamma), (bet, ln_beta)):
                sp.dma_start(dst[:], src.unsqueeze(1)).then_inc(s_w, 16)
            for dst, src in ((cb, conv_b), (dtb, dt_proj_b), (dsk, Dskip)):
                sp.dma_start(dst[:], src.rearrange("(h p) -> p h", p=P)).then_inc(s_w, 16)
            sp.dma_start(kc[:], consts).then_inc(s_w2, 16)
            sp.dma_start(row_list.rearrange("(c p) a -> c (p a)", p=P), spare_rows).then_inc(s_list, 16)
            sp.dma_start(wg_sb[:], Wg).then_inc(s_w2, 16)
            sp.dma_start(bg_rep[:], bg.partition_broadcast(P)).then_inc(s_w2, 16)
            sp.dma_start(w1_sb[:], W1.rearrange("e d h -> d e h")).then_inc(s_w2, 16)
            sp.dma_start(w2_sb[:], W2.rearrange("e (k p) d -> p e k d", p=P)).then_inc(s_w2, 16)
            few.__exit__(None, None, None)
            sp.wait_ge(s_k, 1)
            zeroed = results.rearrange("(n p a) d -> n p (a d)", p=P, a=16)
            for n in range(zeroed.shape[0]):
                sp.dma_start(zeroed[n], free[:, 0:16 * D]).then_inc(s_zres, 16)
            replicate_bc(first)
            stack_parts(first)

            def unit(u, has_prev, has_next):
                if has_next:
                    load_x(u.next())
                    replicate_bc(u.next())
                if has_prev:
                    spill_xn(u.prev())
                if has_next:
                    stack_parts(u.next())
                load_xres(u)

            unit(first, False, True)
            with sp.Fori(0, (UNITS - 2) // 2) as i:
                for k in (1, 2):
                    unit(Unit(i, k), True, True)
            unit(last, True, False)
            sp.wait_ge(s_hc, 8 * UNITS)
            sp.wait_ge(s_st, 8 * UNITS)
            sp.dma_start(b1_rep, b1.rearrange("e h -> (e h)").partition_broadcast(P)).then_inc(s_bias, 16)
            sp.wait_ge(s_y, 8 * UNITS)
            sp.dma_start(b2_rep, b2.rearrange("e d -> (e d)").partition_broadcast(P)).then_inc(s_bias, 16)
            spill_xn(last)
            for b in range(B):
                sp.wait_ge(s_scat[b], 64 * UNITS + 16)
            by_row = row_list.rearrange("(c p) a -> c (p a)", p=P)
            for n in range(3):
                c = min(P, LC - P * n)
                sp.dma_start(lists[0:c, n, :], by_row[P * n:P * n + c, :]).then_inc(s_lists, 16)
            sp.wait_ge(s_spill, 16 * UNITS + 16)
            sp.wait_ge(s_lod, 2 * UNITS)

            def rows(u, plus=0):
                return bass.ds(plus + (T * u.k if u.i is None else u.i * (2 * T) + T * u.k), T)

            def load_sum(u):
                s_in = c_in[u.b]
                passed(c_2, u.value(1, -1))
                sp.dma_start(xcomb[:, u.b], spill[rows(u), :].rearrange("(t p) d -> p t d", p=P)).then_inc(s_in, 16)
                if u.i is None and u.k == 0:
                    for s_ring in e_sc:
                        sp.wait_ge(s_ring, 4 * MAXT)
                for k in range(2):
                    sp.dma_start(ycomb[:, u.b, k],
                                 results[rows(u, NTOK * k), :].rearrange("(t p) d -> p t d", p=P)).then_inc(s_in, 16)

            def store(u):
                passed(s_fin, u.value(1, 1))
                sp.dma_start(out[u.b, bass.ds(u.chunk() * T, T), :].rearrange("(t p) d -> p t d", p=P),
                             final[:, u.b]).then_inc(s_out, 16)

            load_sum(Unit(None, 0))
            load_sum(Unit(None, 1))
            store(Unit(None, 0))
            with sp.Fori(0, (UNITS - 2) // 2) as i:
                for k in (1, 2):
                    load_sum(Unit(i, k + 1))
                    store(Unit(i, k))
            store(Unit(None, UNITS - 1))
            sp.wait_ge(s_out, 16 * UNITS + 16)

        @block.gpsimd
        def _(pool):
            chain = [0]

            def link(ins):
                chain[0] += 1
                ins.then_inc(s_k, 1)
                pool.wait_ge(s_k, chain[0])

            link(nc.gpsimd.memset(hc[:], 0.0))
            link(nc.gpsimd.memset(ident[:], 0.0))
            link(nc.gpsimd.affine_select(out=ident[:], in_=ident[:], compare_op=ALU.not_equal, fill=1.0, base=0,
                                         pattern=[[-1, P]], channel_multiplier=1))
            link(nc.gpsimd.memset(sel[:], 0.0))
            for p in range(3):
                part = sel[32 * p:32 * p + 32, :, :].rearrange("r m (i n) -> r m i n", i=CH)
                link(nc.gpsimd.affine_select(out=part, in_=part, compare_op=ALU.not_equal, fill=1.0, base=0,
                                             pattern=[[-CH, 4], [-1, CH], [0, N]], channel_multiplier=1))
            link(nc.gpsimd.memset(fold[:], 0.0))
            blocks = fold[:].rearrange("p (m c) -> p m c", c=40)[:, :, 0:CH]
            link(nc.gpsimd.memset(blocks, 1.0))
            link(nc.gpsimd.affine_select(out=blocks, in_=blocks, compare_op=ALU.is_ge, fill=0.0, base=0,
                                         pattern=[[0, 4], [-N, CH]], channel_multiplier=1))
            link(nc.gpsimd.affine_select(out=blocks, in_=blocks, compare_op=ALU.is_ge, fill=0.0, base=N - 1,
                                         pattern=[[0, 4], [N, CH]], channel_multiplier=-1))
            link(nc.gpsimd.memset(minus_half[:], -0.5))
            link(nc.gpsimd.memset(ones[:], 1.0))
            link(nc.gpsimd.memset(before[:], 1.0))
            link(nc.gpsimd.affine_select(out=before[:], in_=before[:], compare_op=ALU.is_gt, fill=0.0, base=0,
                                         pattern=[[1, P]], channel_multiplier=-1))

            def power(out_, in_, ready, value, done):
                pool.wait_ge(ready, value)
                nc.gpsimd.tensor_tensor(out_, in_, minus_half[:], ALU.pow).then_inc(done, 1)

            def times_c(u, q):
                pool.wait_ge(s_sc, u.value(32, 4 * q + 4))
                after(pool, s_y, u.value(8, q - 1))
                if q == 0:
                    pool.wait_ge(s_rep[u.b], u.chunk(1) * 256)
                nc.gpsimd.tensor_tensor(hc[:, q % 2], hs[:, q % 2],
                                        Crep[u.b][:].unsqueeze(1).broadcast_to([P, 4, T]),
                                        ALU.mult).then_inc(s_hc, 1)

            def low_delta(u):
                pool.wait_ge(s_r1, u.value(2, 1))
                pool.wait_ge(s_mid, u.value(2, 1))
                nc.gpsimd.tensor_tensor(dpart[2][:], t1[:], dpart[1][:], ALU.subtract).then_inc(s_lod, 2)

            def carry(n):
                return nc.gpsimd.tensor_tensor(carrier[:, n:n + 1], minus_half[:, 0:1], minus_half[:, 0:1], ALU.mult)

            def list_rows(u, t):
                if t == 0:
                    pool.wait_ge(s_pos, u.value(1, 1))
                    carry(8 + u.b)
                for k in range(2):
                    n = 2 * t + k
                    nc.gpsimd.indirect_dma_start(
                        out=row_list, out_offset=bass.IndirectOffsetOnAxis(ap=pos[u.b][:, n:n + 1], axis=0),
                        in_=ids[u.b][:, t, k:k + 1], in_offset=None).then_inc(s_scat[u.b], 16)

            def unit(u, has_prev, has_next):
                if has_next:
                    power(rstd[:], veps[:], s_fve, u.value(1, 2), s_frs)
                if has_prev:
                    times_c(u.prev(), 7)
                for q in range(QUADS - 1):
                    if has_prev:
                        if q == 2:
                            power(crstd[:], cveps[:], s_cve, u.value(1, 0), s_crs)
                        if q == 6:
                            list_rows(u.prev(), 0)
                    if q == 5 and has_next:
                        low_delta(u.next())
                    times_c(u, q)
                if has_prev:
                    for t in range(1, TT):
                        list_rows(u.prev(), t)

            first, last = Unit(None, 0), Unit(None, UNITS - 1)
            for b in range(B):
                nc.gpsimd.dma_start(ids[b][:].rearrange("p t k -> p (t k)"), consts[:, K_AT[b]:K_AT[b + 1]])                    .then_inc(s_scat[b], 16)
            pool.wait_ge(s_list, 16)
            pool.wait_ge(s_zres, 16 * (ROWS // (16 * P)))
            power(rstd[:], veps[:], s_fve, 1, s_frs)
            low_delta(first)
            unit(first, False, True)
            with pool.Fori(0, (UNITS - 2) // 2) as i:
                for k in (1, 2):
                    unit(Unit(i, k), True, True)
            unit(last, True, False)
            times_c(last, 7)
            power(crstd[:], cveps[:], s_cve, UNITS, s_crs)
            for t in range(TT):
                list_rows(last, t)

            def gather(t):
                pool.wait_ge(e_si, t.value(1))
                after(pool, e_xT, t.value(-3))
                after(pool, e_cg, t.value(-3))
                carry(t.ring).then_inc(e_cg, 1)
                nc.gpsimd.indirect_dma_start(
                    out=xg[:, t.ring, :], out_offset=None, in_=spill,
                    in_offset=bass.IndirectOffsetOnAxis(ap=src_now[:, t.ring:t.ring + 1], axis=0)).then_inc(e_g[t.ring], 16)

            def scatter(t):
                pool.wait_ge(e_ob, t.value(1))
                pool.wait_ge(e_di, t.value(1))
                after(pool, e_cs, t.value(-3))
                carry(4 + t.ring).then_inc(e_cs, 1)
                nc.gpsimd.indirect_dma_start(
                    out=results, out_offset=bass.IndirectOffsetOnAxis(ap=dst_now[:, t.ring:t.ring + 1], axis=0),
                    in_=ybuf[:, t.ring, :], in_offset=None).then_inc(e_sc[t.ring], 16)

            def step(n, runs):
                if runs(0):
                    gather(n)
                if runs(7):
                    scatter(n.back(7))

            pool.wait_ge(s_spill, 16 * UNITS + 16)
            pool.wait_ge(s_y, 8 * UNITS)
            tile_steps(pool, step)
            power(frstd[:], fveps[:], s_fv2, 1, s_fr2)
            with pool.Fori(0, (UNITS - 2) // 2) as i:
                for k in (1, 2):
                    power(frstd[:], fveps[:], s_fv2, Unit(i, k).value(1, 1), s_fr2)
            power(frstd[:], fveps[:], s_fv2, UNITS, s_fr2)

        @block.tensor
        def _(pe):
            pe.wait_ge(s_k, 3)
            pe.wait_ge(s_tap, 8)
            for h in range(HALVES):
                for k in range(TAPS):
                    nc.tensor.transpose(bank[h][:, P * k:P * k + P], wtap_raw[:, h, k, :], ident[:])
            for h in range(HALVES):
                nc.tensor.transpose(bank[2][:, P * h:P * h + P], win_raw[:, 2 + h, :], ident[:])
                nc.tensor.transpose(bank[2][:, P * (2 + h):P * (3 + h)], wout_raw[:, P * h:P * h + P], ident[:])
            for h in range(HALVES):
                nc.tensor.transpose(bank[3][:, 96 * h:96 * h + 96], wxp_raw[:, P * h:P * h + P], ident[0:96, 0:96])
                nc.tensor.transpose(bank[3][0:RANK, 256 + P * h:256 + P * h + P], wdt_raw[:, h, :], ident[:])
            nc.tensor.transpose(bank[4][:, 0:32], alog_raw, ident[0:32, 0:32]).then_inc(s_pT, 1)
            pe.wait_ge(s_pe, 7)
            pe.wait_ge(s_k, 14)

            def front_bank(u, use):
                after(pe, s_fd, u.value(8, use - 1))
                return fbanks[use % 2]

            def xhat_T(u):
                o = front_bank(u, 0)
                pe.wait_ge(s_xh, u.value(1, 1))
                for t in range(TT):
                    ins = nc.tensor.transpose(o[:, P * t:P * t + P], xhat[:, t, :], ident[:])
                ins.then_inc(s_ff, 1)

            def conv_u(u, h):
                o = front_bank(u, 1 + 2 * h)
                pe.wait_ge(s_fd, u.value(8, 1))
                for k in range(TAPS):
                    ins = nc.tensor.matmul(o[:], wtapT[:, h, k, :], hT[u.b][:, k:k + T],
                                           start=(k == 0), stop=(k == TAPS - 1))
                ins.then_inc(s_ff, 1)

            def proj_z(u, h):
                o = front_bank(u, 2 + 2 * h)
                nc.tensor.matmul(o[:], wzT[:, h, :], hT[u.b][:, TAPS - 1:]).then_inc(s_ff, 1)

            def proj_x(u):
                o = front_bank(u, 5)
                pe.wait_ge(s_silu, u.value(2, 2))
                for h in range(HALVES):
                    ins = nc.tensor.matmul(o[0:96, :], wxpT[:, h, :], uc[u.b][:, h, :], start=(h == 0), stop=(h == 1))
                ins.then_inc(s_ff, 1)

            def proj_dt(u, h):
                o = front_bank(u, 6 + h)
                pe.wait_ge(s_fd, u.value(8, 6))
                nc.tensor.matmul(o[:], wdtT[:, h, :], xdbl[0:RANK, :]).then_inc(s_ff, 1)

            def replicate(u, g):
                blk, m = 4 * (g // 16) + g % 4, g // 4 % 4
                if g == 0:
                    pe.wait_ge(s_parts[u.b], u.chunk(1) * 384)
                after(pe, s_ex, u.value(32, g - 1))
                nc.tensor.matmul(drep[g % 2][:], sel[:, m, :], dparts[u.b][:, blk, :]).then_inc(s_dr, 1)
                after(pe, s_bu, u.value(32, g - 1))
                nc.tensor.matmul(urep[g % 2][:], sel[:, m, :], uparts[u.b][:, blk, :]).then_inc(s_ur, 1)

            def add_states(u, q):
                pe.wait_ge(s_hc, u.value(8, q + 1))
                if q % 4 == 0:
                    after(pe, s_yd, u.value(2, q // 4))
                m = q % 4
                for j in range(4):
                    ins = nc.tensor.matmul(ybank[32 * j:32 * j + 32, :], fold[:, 32 * m:32 * m + 32], hc[:, q % 2, j, :],
                                           start=(m == 0), stop=(m == 3))
                ins.then_inc(s_y, 1)

            def m_bank(u, use):
                pe.wait_ge(s_md, u.value(4, MUSES.index(use) + 1))
                return mbank

            def out_proj(u):
                o = m_bank(u, "oproj")
                pe.wait_ge(s_yg, u.value(2, 2))
                for t in range(TT):
                    for h in range(HALVES):
                        ins = nc.tensor.matmul(o[:, P * t:P * t + P], yg[:, h, P * t:P * t + P], woutT[:, h, :],
                                               start=(h == 0), stop=(h == 1))
                ins.then_inc(s_mf, 1)

            def xn_T(u):
                o = m_bank(u, "xnT")
                pe.wait_ge(s_xn, u.value(1, 1))
                for t in range(TT):
                    ins = nc.tensor.transpose(o[:, P * t:P * t + P], xn[:, t, :], ident[:])
                ins.then_inc(s_mf, 1)

            def logits(u):
                o = m_bank(u, "logits")
                for t in range(TT):
                    ins = nc.tensor.matmul(o[:, E * t:E * t + E], xnT[:, P * t:P * t + P], wg_sb[:])
                ins.then_inc(s_mf, 1)

            def ranks(u):
                o = m_bank(u, "rank")
                pe.wait_ge(s_gate, u.value(GATE, 5))
                for t in range(TT + 1):
                    oo = o[:, E * t:E * t + E]
                    for s in range(t):
                        ins = nc.tensor.matmul(oo, ones[:], taken[:, s, :], start=(s == 0), stop=(t == TT and s == TT - 1))
                    if t < TT:
                        nc.tensor.matmul(oo, before[:], taken[:, t, :], start=(t == 0), stop=True)
                ins.then_inc(s_mf, 1)

            front = {3: lambda u: xhat_T(u), 4: lambda u: conv_u(u, 0), 5: lambda u: proj_z(u, 0),
                     6: lambda u: conv_u(u, 1), 7: lambda u: proj_z(u, 1), 12: lambda u: proj_x(u),
                     13: lambda u: proj_dt(u, 0), 14: lambda u: proj_dt(u, 1)}
            back = {2: lambda u: add_states(u, 6), 5: lambda u: add_states(u, 7), 8: out_proj,
                    15: xn_T, 17: logits, 20: ranks}

            def unit(u, has_prev, has_next):
                for g in range(4 * QUADS):
                    replicate(u, g)
                    if g >= 10 and g % 4 == 2:
                        add_states(u, g // 4 - 2)
                    if has_next and g in front:
                        front[g](u.next())
                    if has_prev and g in back:
                        back[g](u.prev())

            first, last = Unit(None, 0), Unit(None, UNITS - 1)
            for g in sorted(front):
                front[g](first)
            pe.wait_ge(s_w2, 80)
            unit(first, False, True)
            with pe.Fori(0, (UNITS - 2) // 2) as i:
                for k in (1, 2):
                    unit(Unit(i, k), True, True)
            unit(last, True, False)
            for g in sorted(back):
                back[g](last)

            pe.wait_ge(s_lists, 48)
            pe.wait_ge(s_plan, 12)
            for n in range(3):
                c = min(P, LC - P * n)
                ins = nc.tensor.matmul(mbank[:, 0:MAXT], lists[0:c, n, :], pick[0:c, n, :], start=(n == 0), stop=(n == 2))
            ins.then_inc(s_pick, 1)

            def x_T(t):
                pe.wait_ge(e_g[t.ring], t.dmas(1))
                after(pe, e_xe, t.value(-1))
                nc.tensor.transpose(xT_banks[t.ring % 2][:, 0:P], xg[:, t.ring, :], ident[:]).then_inc(e_xT, 1)

            def hidden(t):
                e = pe.value_load(etab[0:1, t.at()], min_val=0, max_val=E - 1)
                pe.wait_ge(e_xe, t.value(1))
                after(pe, e_hb, t.value(-1))
                nc.tensor.matmul(h_banks[t.ring % 2][:], xTs[:, t.ring % 2, :],
                                 w1_sb[:].rearrange("p e h -> p (e h)")[:, bass.ds(e * H, H)]).then_inc(e_h, 1)

            def hidden_T(t):
                pe.wait_ge(e_hb, t.value(1))
                after(pe, e_ge, t.value(-1))
                for k in range(HK):
                    ins = nc.tensor.transpose(hT_banks[t.ring % 2][:, P * k:P * k + P],
                                              hbuf[:, t.ring % 2, P * k:P * k + P], ident[:])
                ins.then_inc(e_hT, 1)

            def output(t):
                e = pe.value_load(etab[0:1, t.at()], min_val=0, max_val=E - 1)
                pe.wait_ge(e_ge, t.value(1))
                after(pe, e_ob, t.value(-1))
                for k in range(HK):
                    ins = nc.tensor.matmul(o_banks[t.ring % 2][:, 0:D], hTs[:, t.ring % 2, P * k:P * k + P],
                                           w2_sb[:].rearrange("p e k d -> p (e k d)")[:, bass.ds(e * (HK * D) + k * D, D)],
                                           start=(k == 0), stop=(k == HK - 1))
                ins.then_inc(e_o, 1)

            def step(n, runs):
                if runs(3):
                    x_T(n.back(3))
                if runs(4):
                    hidden(n.back(4))
                if runs(5):
                    hidden_T(n.back(5))
                if runs(6):
                    output(n.back(6))

            tile_steps(pe, step)

        @block.scalar
        def _(act):
            act.wait_ge(s_pT, 1)
            for h in range(HALVES):
                nc.scalar.copy(wtapT[:, h].rearrange("p k c -> p (k c)"), bank[h][:]).then_inc(s_pe, 1)
            nc.scalar.copy(wzT[:].rearrange("p h c -> p (h c)"), bank[2][:, 0:256]).then_inc(s_pe, 1)
            nc.scalar.copy(woutT[:].rearrange("p h c -> p (h c)"), bank[2][:, 256:512]).then_inc(s_pe, 1)
            nc.scalar.copy(wxpT[:].rearrange("p h c -> p (h c)"), bank[3][:, 0:192]).then_inc(s_pe, 1)
            nc.scalar.copy(wdtT[:].rearrange("p h c -> p (h c)"), bank[3][0:RANK, 256:512]).then_inc(s_pe, 1)
            nc.scalar.activation(aexp[:], bank[4][:, 0:32], ACT.Exp).then_inc(s_pe, 1)

            def filled(u, use):
                act.wait_ge(s_ff, u.value(8, use + 1))

            def h_evac(u):
                nc.scalar.copy(hT[u.b][:, 0:TAPS - 1], hT[u.b][:, T:]).then_inc(s_carry, 1)
                act.wait_ge(s_carry, u.value(1, 1))
                filled(u, 0)
                nc.scalar.activation(hT[u.b][:, TAPS - 1:], fbanks[0][:], ACT.Identity, bias=bet[:], scale=gam[:])\
                    .then_inc(s_fd, 1)

            def u_evac(u, h):
                filled(u, 1 + 2 * h)
                after(act, s_lod, u.value(2, 0))
                after(act, s_lo, u.value(2, 0))
                nc.scalar.activation(pre[:, 2 * h, :], fbanks[1][:], ACT.Identity, bias=cb[:, h:h + 1]).then_inc(s_fd, 1)

            def z_evac(u, h):
                filled(u, 2 + 2 * h)
                nc.scalar.activation(pre[:, 2 * h + 1, :], fbanks[0][:], ACT.Copy).then_inc(s_fd, 1)

            def silus(u):
                act.wait_ge(s_fd, u.value(8, 5))
                after(act, s_yd, u.value(2, -2))
                after(act, s_yg, u.value(2, -2))
                nc.scalar.activation(uc[u.b][:], pre[:, 0:4:2, :], ACT.Silu).then_inc(s_silu, 1)
                nc.scalar.activation(sz[u.b][:], pre[:, 1:4:2, :], ACT.Silu).then_inc(s_silu, 1)

            def xdbl_evac(u):
                filled(u, 5)
                after(act, s_rep[1 - u.b], u.prev().chunk(1) * 256 if (u.i is not None or u.k) else 0)
                nc.scalar.copy(xdbl[:], fbanks[1][0:96, :]).then_inc(s_fd, 1)

            def dt_evac(u, h):
                filled(u, 6 + h)
                o = fbanks[h]
                nc.scalar.activation(t1[:, h, :], o[:], ACT.Abs, bias=dtb[:, h:h + 1]).then_inc(s_abs, 1)
                nc.scalar.activation(t4[:, h, :], o[:], ACT.Relu, bias=dtb[:, h:h + 1]).then_inc(s_fd, 1)

            def exponential(u):
                act.wait_ge(s_abs, u.value(2, 2))
                nc.scalar.activation(t1[:], t1[:], ACT.Exp, scale=-1.0).then_inc(s_e, 1)

            def logarithm(u):
                act.wait_ge(s_1pe, u.value(1, 1))
                nc.scalar.activation(t3[:], t2[:], ACT.Ln).then_inc(s_ln, 1)

            def hi_part(u, n):
                if n == 0:
                    after(act, s_parts[1 - u.b], u.prev().chunk(1) * 384 if (u.i is not None or u.k) else 0)
                act.wait_ge((s_delta, s_du)[n], u.value(1, 1))
                nc.scalar.copy((dpart, upart)[n][0][:], (t3, t4)[n][:]).then_inc(s_hi, 1)

            def mid_part(u, n):
                act.wait_ge(s_r1, u.value(2, n + 1))
                nc.scalar.copy((dpart, upart)[n][1][:], (t1, t2)[n][:]).then_inc(s_mid, 1)

            def decays(u, g):
                act.wait_ge(s_dr, u.value(32, g + 1))
                after(act, s_sc, u.value(32, g - 3))
                ch = tile_of(g // 4, g % 4)
                nc.scalar.activation(decay[:, g % 4, :], drep[g % 2][:], ACT.Exp, scale=negA[:, ch:ch + 1]).then_inc(s_ex, 1)

            def xnT_evac(u):
                act.wait_ge(s_mf, u.value(4, 2))
                nc.scalar.copy(xnT[:], mbank[:]).then_inc(s_md, 1)

            def gate_exp(u):
                act.wait_ge(s_gate, u.value(GATE, 2))
                nc.scalar.activation(ex[:], ex[:], ACT.Exp).then_inc(s_gex, 1)

            front = {3: h_evac, 5: lambda u: u_evac(u, 0), 6: lambda u: z_evac(u, 0), 7: lambda u: u_evac(u, 1),
                     8: lambda u: z_evac(u, 1), 9: silus, 12: xdbl_evac, 13: lambda u: dt_evac(u, 0),
                     14: lambda u: dt_evac(u, 1), 15: exponential, 17: logarithm, 20: lambda u: hi_part(u, 0),
                     22: lambda u: (hi_part(u, 1), mid_part(u, 0)), 24: lambda u: mid_part(u, 1)}
            back = {14: xnT_evac, 18: gate_exp}

            def unit(u, has_prev, has_next):
                for g in range(4 * QUADS):
                    decays(u, g)
                    if has_next and g in front:
                        front[g](u.next())
                    if has_prev and g in back:
                        back[g](u.prev())

            first, last = Unit(None, 0), Unit(None, UNITS - 1)
            act.wait_ge(s_zero, 3)
            for g in sorted(front):
                front[g](first)
            act.wait_ge(s_negA, 1)
            unit(first, False, True)
            with act.Fori(0, (UNITS - 2) // 2) as i:
                for k in (1, 2):
                    unit(Unit(i, k), True, True)
            unit(last, True, False)
            for g in sorted(back):
                back[g](last)

            def x_evac(t):
                act.wait_ge(e_xT, t.value(1))
                after(act, e_h, t.value(-1))
                nc.scalar.copy(xTs[:, t.ring % 2, :], xT_banks[t.ring % 2][:, 0:P]).then_inc(e_xe, 1)

            def gelu(t):
                act.wait_ge(e_hT, t.value(1))
                after(act, e_o, t.value(-1))
                nc.scalar.activation(hTs[:, t.ring % 2, :], hT_banks[t.ring % 2][:], ACT.Gelu).then_inc(e_ge, 1)

            def step(n, runs):
                if runs(3):
                    x_evac(n.back(3))
                if runs(5):
                    gelu(n.back(5))

            act.wait_ge(s_y, 8 * UNITS)
            tile_steps(act, step)

        @block.vector
        def _(dve):
            nc.vector.memset(state[:], 0.0).then_inc(s_zero, 1)
            for b in range(B):
                nc.vector.memset(hT[b][:, T:], 0.0).then_inc(s_zero, 1)
            dve.wait_ge(s_w, 16 * 11)
            for h in range(HALVES):
                for k in range(TAPS):
                    nc.vector.tensor_scalar(wtap_raw[:, h, k, :], win_raw[:, h, :], cw[:, h, k:k + 1], None,
                                            ALU.mult).then_inc(s_tap, 1)
            dve.wait_ge(s_pe, 7)
            nc.vector.tensor_scalar(negA[:], aexp[:], -1.0, None, ALU.mult).then_inc(s_negA, 1)

            def moments(u, src, st, mvar, ve, eps, s1, s2, s3):
                for t in range(TT):
                    ins = nc.vector.bn_stats(st[:, t, :], src[:, t, :])
                ins.then_inc(s1, 1)
                dve.wait_ge(s1, u.value(1, 1))
                nc.vector.tensor_copy(zero2[:], zero2[:])
                for t in range(TT):
                    ins = nc.vector.bn_aggr(mvar[:, t, :], st[:, t, :])
                ins.then_inc(s2, 1)
                dve.wait_ge(s2, u.value(1, 1))
                nc.vector.tensor_scalar(ve[:], mvar[:, :, 1], eps, None, ALU.add).then_inc(s3, 1)

            def normalise(u, dst, src, mvar, rs, ready, done):
                dve.wait_ge(ready, u.value(1, 1))
                for t in range(TT):
                    ins = nc.vector.tensor_scalar(dst[:, t, :], src[:, t, :], mvar[:, t, 0:1], rs[:, t:t + 1],
                                                  ALU.subtract, ALU.mult)
                ins.then_inc(done, 1)

            def front_stats(u):
                dve.wait_ge(s_x[u.b], u.chunk(1) * 16)
                moments(u, xin[u.b], bst, mv, veps, 1e-6, s_fst, s_fag, s_fve)

            def front_norm(u):
                after(dve, s_ff, u.value(8, -7))
                normalise(u, xhat, xin[u.b], mv, rstd, s_frs, s_xh)

            def one_plus_e(u):
                dve.wait_ge(s_e, u.value(1, 1))
                nc.vector.tensor_scalar(t2[:], t1[:], 1.0, None, ALU.add).then_inc(s_1pe, 1)

            def softplus(u):
                dve.wait_ge(s_ln, u.value(1, 1))
                nc.vector.scalar_tensor_tensor(t2[:], t2[:], 1.0, t1[:], ALU.subtract, ALU.subtract).then_inc(s_nc, 1)
                dve.wait_ge(s_nc, u.value(1, 1))
                nc.vector.tensor_tensor(t3[:], t3[:], t2[:], ALU.subtract).then_inc(s_l1p, 1)
                dve.wait_ge(s_l1p, u.value(2, 1))
                nc.vector.tensor_tensor(t3[:], t3[:], t1[:], ALU.min).then_inc(s_l1p, 1)
                dve.wait_ge(s_l1p, u.value(2, 2))
                nc.vector.tensor_tensor(t3[:], t3[:], t4[:], ALU.add).then_inc(s_delta, 1)

            def delta_u(u):
                dve.wait_ge(s_delta, u.value(1, 1))
                nc.vector.tensor_tensor(t4[:], t3[:], uc[u.b][:], ALU.mult).then_inc(s_du, 1)

            def rest(u, n):
                dve.wait_ge(s_hi, u.value(2, n + 1))
                dst, src, part = ((t1, t3, dpart), (t2, t4, upart))[n]
                nc.vector.tensor_tensor(dst[:], src[:], part[0][:], ALU.subtract).then_inc(s_r1, 1)

            def low_du(u):
                dve.wait_ge(s_r1, u.value(2, 2))
                dve.wait_ge(s_mid, u.value(2, 2))
                nc.vector.tensor_tensor(upart[2][:], t2[:], upart[1][:], ALU.subtract).then_inc(s_lo, 2)

            def inflows(u, g):
                dve.wait_ge(s_ur, u.value(32, g + 1))
                if g == 0:
                    dve.wait_ge(s_rep[u.b], u.chunk(1) * 256)
                after(dve, s_sc, u.value(32, g - 1))
                nc.vector.tensor_tensor(inflow[:, g % 2, :], urep[g % 2][:], Brep[u.b][:], ALU.mult).then_inc(s_bu, 1)

            def keep(u, q):
                dve.wait_ge(s_sc, u.value(32, 4 * q + 4))
                nc.vector.tensor_copy(state[:, u.b, q // 4, q % 4, :], hs[:, q % 2, :, T - 1]).then_inc(s_st, 1)

            def scan(u, g):
                q, j = g // 4, g % 4
                dve.wait_ge(s_ex, u.value(32, g + 1))
                dve.wait_ge(s_bu, u.value(32, g + 1))
                if j == 0:
                    after(dve, s_hc, u.value(8, q - 1))
                    after(dve, s_st, u.value(8, q - 1))
                nc.vector.tensor_tensor_scan(hs[:, q % 2, j, :], decay[:, j, :], inflow[:, g % 2, :],
                                             state[:, u.b, q // 4, q % 4, j:j + 1], ALU.mult, ALU.add).then_inc(s_sc, 1)

            def post(u, h):
                dve.wait_ge(s_y, u.value(8, 4 * h + 4))
                nc.vector.scalar_tensor_tensor(yg[:, h, :], uc[u.b][:, h, :], dsk[:, h:h + 1], ybank[:],
                                               ALU.mult, ALU.add).then_inc(s_yd, 1)
                dve.wait_ge(s_yd, u.value(2, h + 1))
                nc.vector.tensor_tensor(yg[:, h, :], yg[:, h, :], sz[u.b][:, h, :], ALU.mult).then_inc(s_yg, 1)

            def residual(u):
                dve.wait_ge(s_mf, u.value(4, 1))
                dve.wait_ge(s_xr, u.value(16, 16))
                nc.vector.scalar_tensor_tensor(res[:].rearrange("p t d -> p (t d)"),
                                               xres[:].rearrange("p t d -> p (t d)"), 2.0, mbank[:],
                                               ALU.mult, ALU.add).then_inc(s_md, 1)
                dve.wait_ge(s_md, u.value(4, 2))
                nc.vector.tensor_copy(zero2[:], res[:, 0, 0:1]).then_inc(s_res, 1)
                moments(u, res, cst, cmv, cveps, 1e-5, s_cst, s_cag, s_cve)

            def norm1(u):
                dve.wait_ge(s_spill, u.value(16, 16))
                normalise(u, xn, res, cmv, crstd, s_crs, s_xn)

            def at(u, n):
                return u.value(GATE, n)

            def gate(u):
                dve.wait_ge(s_mf, u.value(4, 3))
                nc.vector.tensor_tensor(lg[:], mbank[:, 0:TT * E].rearrange("p (t e) -> p t e", e=E),
                                        bg_rep[:].unsqueeze(1).broadcast_to([P, TT, E]), ALU.add).then_inc(s_md, 1)
                dve.wait_ge(s_md, u.value(4, 4))
                nc.vector.tensor_copy(zero2[:], zero2[:])
                for t in range(TT):
                    ins = nc.vector.max(top[:, t, :], lg[:, t, :])
                ins.then_inc(s_gate, 1)
                dve.wait_ge(s_gate, at(u, 1))
                nc.vector.tensor_tensor(ex[:], top[:], top[:, :, 0:1].broadcast_to([P, TT, E]),
                                        ALU.subtract).then_inc(s_gate, 1)
                for t in range(TT):
                    ins = nc.vector.max_index(topi[:, t, :], top[:, t, :], lg[:, t, :])
                ins.then_inc(s_gate, 1)
                dve.wait_ge(s_gate, at(u, 3))
                nc.vector.tensor_copy(topf[:], topi[:, :, 0:2]).then_inc(s_gate, 1)
                dve.wait_ge(s_gate, at(u, 4))
                for k in range(2):
                    ins = nc.vector.tensor_tensor(oh[:, :, k, :], lane.unsqueeze(1).broadcast_to([P, TT, E]),
                                                  topf[:, :, k:k + 1].broadcast_to([P, TT, E]), ALU.is_equal)
                ins.then_inc(s_oh, 1)
                dve.wait_ge(s_oh, u.value(1, 1))
                nc.vector.tensor_tensor(taken[:], oh[:, :, 0, :], oh[:, :, 1, :], ALU.add).then_inc(s_gate, 1)

            def place(u):
                dve.wait_ge(s_gex, u.value(1, 1))
                nc.vector.reduce_sum(esum[:], ex[:], AX_X).then_inc(s_gate, 1)
                dve.wait_ge(s_gate, at(u, 6))
                nc.vector.reciprocal(erec[:], esum[:]).then_inc(s_gate, 1)
                dve.wait_ge(s_gate, at(u, 7))
                w = 2 * TT
                here = bass.ds(w * u.k if u.i is None else u.i * (2 * w) + w * u.k, w)
                nc.vector.tensor_tensor(probs[:, here].rearrange("p (t k) -> p t k", k=2), ex[:, :, 0:2],
                                        erec[:].unsqueeze(2).broadcast_to([P, TT, 2]), ALU.mult).then_inc(s_gate, 1)
                dve.wait_ge(s_mf, u.value(4, 4))
                counts = mbank[:, 0:(TT + 1) * E].rearrange("p (t e) -> p t e", e=E)
                nc.vector.tensor_tensor(rank[:], counts[:, 0:TT, :], run[:].unsqueeze(1).broadcast_to([P, TT, E]),
                                        ALU.add).then_inc(s_gate, 1)
                dve.wait_ge(s_gate, at(u, 9))
                nc.vector.tensor_tensor(run[:], run[:], counts[:, TT, :], ALU.add).then_inc(s_md, 1)
                for k in range(2):
                    ins = nc.vector.tensor_tensor(masked[:, :, k, :], oh[:, :, k, :], rank[:], ALU.mult)
                ins.then_inc(s_gate, 1)
                dve.wait_ge(s_gate, at(u, 10))
                nc.vector.reduce_sum(posf[:].rearrange("p t k -> p (t k)"), masked[:].rearrange("p t k e -> p (t k) e"),
                                     AX_X).then_inc(s_gate, 1)
                dve.wait_ge(s_scat[u.b], u.chunk() * 128 + 16)
                nc.vector.tensor_scalar(ids[u.b][:], ids[u.b][:], 2.0 * T, None, ALU.add).then_inc(s_gate, 1)
                dve.wait_ge(s_gate, at(u, 11))
                nc.vector.tensor_copy(pos[u.b][:], posf[:].rearrange("p t k -> p (t k)")).then_inc(s_gate, 1)
                dve.wait_ge(s_gate, at(u, 13))
                dve.sem_inc(s_pos, 1)

            front = {0: front_stats, 1: front_norm, 16: one_plus_e, 18: softplus, 21: delta_u,
                     22: lambda u: rest(u, 0), 23: lambda u: rest(u, 1), 25: low_du}
            back = {6: lambda u: post(u, 1), 8: residual, 13: norm1, 18: gate, 22: place}

            def unit(u, has_prev, has_next):
                for g in range(4 * QUADS):
                    if g == 0:
                        inflows(u, 0)
                    if g < 31:
                        inflows(u, g + 1)
                    if g % 4 == 0 and g > 0:
                        keep(u, g // 4 - 1)
                    scan(u, g)
                    if has_next and g in front:
                        front[g](u.next())
                    if has_prev and g in back:
                        back[g](u.prev())
                    if g == 23:
                        post(u, 0)
                keep(u, QUADS - 1)

            first, last = Unit(None, 0), Unit(None, UNITS - 1)
            nc.vector.memset(zero2[:], 0.0).then_inc(s_zero, 1)
            dve.wait_ge(s_zero, 4)
            dve.sem_inc(s_md, 1)
            dve.sem_inc(s_spill, 16)
            dve.sem_inc(s_out, 16)
            for g in sorted(front):
                front[g](first)
            dve.wait_ge(s_w2, 80)
            nc.vector.tensor_copy(run[:], base).then_inc(s_zero, 1)
            dve.wait_ge(s_zero, 5)
            unit(first, False, True)
            with dve.Fori(0, (UNITS - 2) // 2) as i:
                for k in (1, 2):
                    unit(Unit(i, k), True, True)
            unit(last, True, False)
            for g in sorted(back):
                back[g](last)

            planned = [0]

            def plan(ins):
                planned[0] += 1
                ins.then_inc(s_plan, 1)
                dve.wait_ge(s_plan, planned[0])

            dve.wait_ge(s_md, 4 * UNITS + 1)
            plan(nc.vector.tensor_tensor(count[:], run[:], base, ALU.subtract))
            plan(nc.vector.tensor_tensor(over, count[:].unsqueeze(2).broadcast_to([P, E, NTOK // P]),
                                         thresholds.unsqueeze(1).broadcast_to([P, E, NTOK // P]), ALU.is_gt))
            plan(nc.vector.reduce_sum(tiles[:], over, AX_X))
            plan(nc.vector.tensor_tensor_scan(cum[:], one8, tiles[:],
                                              0.0, ALU.mult, ALU.add))
            cums = cum[:].unsqueeze(1).broadcast_to([P, MAXT, E])
            plan(nc.vector.tensor_tensor(past, numbers.unsqueeze(2).broadcast_to([P, MAXT, E]), cums, ALU.is_ge))
            plan(nc.vector.tensor_tensor(pastc, past, cums, ALU.mult))
            plan(nc.vector.reduce_sum(region[:], past, AX_X))
            plan(nc.vector.reduce_max(start[:], pastc, AX_X))
            plan(nc.vector.tensor_tensor(within[:], numbers, start[:], ALU.subtract))
            plan(nc.vector.scalar_tensor_tensor(lrow[:], region[:], float(NTOK // P), within[:], ALU.mult, ALU.add))
            plan(nc.vector.tensor_scalar(expert[:], region[:], float(E - 1), None, ALU.min))
            for n in range(3):
                ins = nc.vector.tensor_scalar(pick[:, n, :], lrow[:], rows_of[:, n:n + 1], None, ALU.is_equal)
            plan(ins)
            plan(nc.vector.tensor_copy(etab[:], expert[:]))
            dve.wait_ge(s_pick, 1)
            plan(nc.vector.tensor_copy(dstf[:], mbank[:, 0:MAXT]))
            plan(nc.vector.tensor_copy(dst_tab[:], dstf[:]))
            plan(nc.vector.tensor_scalar(fix1[:], dstf[:], float(NTOK), -float(NTOK), ALU.is_ge, ALU.mult))
            plan(nc.vector.tensor_scalar(fix2[:], dstf[:], float(2 * NTOK), -float(NTOK), ALU.is_ge, ALU.mult))
            plan(nc.vector.tensor_tensor(fix1[:], fix1[:], fix2[:], ALU.add))
            plan(nc.vector.tensor_tensor(srcf[:], dstf[:], fix1[:], ALU.add))
            plan(nc.vector.tensor_copy(src_tab[:], srcf[:]))

            def source(t):
                after(dve, e_g[t.ring], t.dmas(0))
                nc.vector.tensor_copy(src_now[:, t.ring:t.ring + 1], src_tab[:, t.at()]).then_inc(e_si, 1)

            def hidden_bias(t):
                e = dve.value_load(etab[0:1, t.at()], min_val=0, max_val=E - 1)
                dve.wait_ge(e_h, t.value(1))
                after(dve, e_hT, t.value(-1))
                nc.vector.tensor_tensor(hbuf[:, t.ring % 2, :], h_banks[t.ring % 2][:], b1_rep[:, bass.ds(e * H, H)],
                                        ALU.add).then_inc(e_hb, 1)

            def output_bias(t):
                e = dve.value_load(etab[0:1, t.at()], min_val=0, max_val=E - 1)
                dve.wait_ge(e_o, t.value(1))
                after(dve, e_sc[t.ring], t.dmas(0))
                nc.vector.tensor_tensor(ybuf[:, t.ring, :], o_banks[t.ring % 2][:, 0:D], b2_rep[:, bass.ds(e * D, D)],
                                        ALU.add).then_inc(e_ob, 1)
                nc.vector.tensor_copy(dst_now[:, t.ring:t.ring + 1], dst_tab[:, t.at()]).then_inc(e_di, 1)

            def step(n, runs):
                if runs(0):
                    source(n)
                if runs(4):
                    hidden_bias(n.back(4))
                if runs(6):
                    output_bias(n.back(6))

            dve.wait_ge(s_bias, 32)
            tile_steps(dve, step)

            def add_experts(u):
                w = 2 * TT
                here = bass.ds(w * u.k if u.i is None else u.i * (2 * w) + w * u.k, w)
                nc.vector.tensor_copy(pcur[:, u.b].rearrange("p t k -> p (t k)"), probs[:, here]).then_inc(c_p, 1)
                dve.wait_ge(c_p, u.value(1, 1))
                dve.wait_ge(c_in[u.b], u.chunk(1) * 48)
                for k in range(2):
                    for t in range(TT):
                        ins = nc.vector.scalar_tensor_tensor(
                            total[:, u.b, t, :], ycomb[:, u.b, k, t, :], pcur[:, u.b, t, k:k + 1],
                            xcomb[:, u.b, t, :] if k == 0 else total[:, u.b, t, :], ALU.mult, ALU.add)
                    ins.then_inc((c_1, c_2)[k], 1)
                    dve.wait_ge((c_1, c_2)[k], u.value(1, 1))
                moments(u, total[:, u.b], fst, fmv, fveps, 1e-5, s_fs2, s_fa2, s_fv2)

            def norm2(u):
                after(dve, s_out, u.value(16, 0))
                normalise(u, final[:, u.b], total[:, u.b], fmv, frstd, s_fr2, s_fin)

            for u in (Unit(None, 0), ):
                add_experts(u)
                norm2(u)
            with dve.Fori(0, (UNITS - 2) // 2) as i:
                for k in (1, 2):
                    add_experts(Unit(i, k))
                    norm2(Unit(i, k))
            add_experts(Unit(None, UNITS - 1))
            norm2(Unit(None, UNITS - 1))


_INS = ["L0_attn_x", "L0_attn_ln_gamma", "L0_attn_ln_beta", "L0_attn_in_proj_w", "L0_attn_conv_w", "L0_attn_conv_b",
        "L0_attn_x_proj_w", "L0_attn_dt_proj_w", "L0_attn_dt_proj_b", "L0_attn_A_log", "L0_attn_D",
        "L0_attn_out_proj_w", "L0_ffn_Wg", "L0_ffn_bg", "L0_ffn_W1", "L0_ffn_b1", "L0_ffn_W2", "L0_ffn_b2"]


K_PARTS = [2 * TT, 2 * TT, E, NTOK // P, MAXT, 3, E, E]
K_AT = [sum(K_PARTS[:n]) for n in range(len(K_PARTS) + 1)]
CONSTS = K_AT[-1]


def kernel(**inputs):
    import numpy as np
    import concourse.bacc as bacc
    from concourse.bass_utils import run_bass_kernel_spmd

    nc = bacc.Bacc("TRN2", target_bir_lowering=False, num_devices=1)
    arrays, args = {}, []
    for name in _INS:
        a = np.ascontiguousarray(inputs[name])
        arrays[name] = a
        args.append(nc.dram_tensor(name, a.shape, mybir.dt.from_np(a.dtype), kind="ExternalInput").ap())
    p = np.arange(P)[:, None]
    first_rows = p + P * np.arange(TT).repeat(2)[None] + NTOK * np.tile([0, 1], TT)[None]
    wide = [first_rows - 2 * T, first_rows - T, np.arange(E)[None] * NTOK + 0 * p, np.arange(NTOK // P)[None] * P + 0 * p,
            np.arange(MAXT)[None] + 0 * p, p + P * np.arange(3)[None], np.arange(E)[None] + 0 * p, 1 + 0 * p + np.zeros((1, E))]
    arrays["consts"] = np.concatenate(wide, 1).astype(np.float32)
    c = np.arange(LC)[:, None]
    spare = np.where(c < LC - E, c // (NTOK // P), c - (LC - E) + E)
    arrays["spare_rows"] = (2 * NTOK + P * spare + np.arange(P)[None]).astype(np.float32)
    made = [nc.dram_tensor(n, arrays[n].shape, F32, kind="ExternalInput").ap() for n in ("consts", "spare_rows")]
    spill = nc.dram_tensor("spill", (NTOK, D), F32, kind="Internal").ap()
    row_list = nc.dram_tensor("row_list", (LIST, 1), F32, kind="Internal").ap()
    results = nc.dram_tensor("results", (ROWS, D), F32, kind="Internal").ap()
    out = nc.dram_tensor("out", (B, L, D), F32, kind="ExternalOutput").ap()
    mamba_moe(nc, *made, spill, row_list, results, *args, out)
    r = run_bass_kernel_spmd(nc, [arrays], core_ids=[0])
    return r.results[0]["out"]
```

```python
from contextlib import ExitStack

import concourse.bass as bass
from concourse import mybir

ALU = mybir.AluOpType
ACT = mybir.ActivationFunctionType
BF16 = mybir.dt.bfloat16
F32 = mybir.dt.float32
U32 = mybir.dt.uint32
AX_X = mybir.AxisListType.X

P = 128
B, L, D = 2, 2048, 128
DI, N, RANK, TAPS = 256, 16, 64, 4
E, H = 8, 512
T = 512
UNITS = B * L // T
TT = T // P
HALVES = DI // P
CH = P // N
QUADS = 8
HK = H // P
NTOK = B * L
MAXT = 2 * NTOK // P + E
LIST = E * NTOK + E * P
LC = LIST // P
ROWS = 2 * NTOK + 2 * E * P


class Unit:

    def __init__(self, i, k):
        self.i, self.k, self.b = i, k, k % 2

    def value(self, per_unit, plus):
        fixed = per_unit * self.k + plus
        if self.i is None:
            return fixed
        assert fixed > 0
        return self.i * (2 * per_unit) + fixed

    def chunk(self, plus=0):
        c = self.k // 2 + plus
        return c if self.i is None else self.i + c

    def next(self):
        return Unit(self.i, self.k + 1)

    def prev(self):
        return Unit(self.i, self.k - 1)


class Tile:

    def __init__(self, i, k):
        self.i, self.k, self.ring = i, k, k % 4

    def value(self, plus, scale=1):
        fixed = scale * (self.k + plus)
        if self.i is None:
            return fixed
        assert fixed > 0
        return self.i * (4 * scale) + fixed

    def dmas(self, plus):
        fixed = 16 * (self.k // 4 + plus)
        return fixed if self.i is None else self.i * 16 + fixed

    def at(self, size=1):
        fixed = self.k * size
        return bass.ds(fixed if self.i is None else self.i * (4 * size) + fixed, size)

    def back(self, lag):
        return Tile(self.i, self.k - lag)


def mamba_moe(nc, consts, spare_rows, spill, row_list, results, x, ln_gamma, ln_beta, in_proj_w, conv_w, conv_b, x_proj_w, dt_proj_w, dt_proj_b,
              A_log, Dskip, out_proj_w, Wg, bg, W1, b1, W2, b2, out):
    with ExitStack() as ctx:
        def sb(name, shape, dt=F32):
            return ctx.enter_context(nc.sbuf_tensor(name, shape, dt))

        def sem(name):
            return ctx.enter_context(nc.semaphore(name))

        def after(eng, semaphore, value):
            if isinstance(value, int) and value <= 0:
                return
            eng.wait_ge(semaphore, value)

        ident = sb("ident", [P, P])
        sel = sb("sel", [96, 4, P], BF16)
        fold = sb("fold", [P, 160])
        wtapT = sb("wtapT", [P, HALVES, TAPS, P])
        wzT = sb("wzT", [P, HALVES, P])
        woutT = sb("woutT", [P, HALVES, D])
        wxpT = sb("wxpT", [P, HALVES, RANK + 2 * N])
        wdtT = sb("wdtT", [RANK, HALVES, P])
        negA = sb("negA", [P, DI * N // P])
        aexp = sb("aexp", [P, DI * N // P])
        gam = sb("gam", [P, 1])
        bet = sb("bet", [P, 1])
        cw = sb("cw", [P, HALVES, TAPS])
        cb = sb("cb", [P, HALVES])
        dtb = sb("dtb", [P, HALVES])
        dsk = sb("dsk", [P, HALVES])
        skip = sb("skip", [P, HALVES, P])
        wg_sb = sb("wg_sb", [P, E])
        bg_rep = sb("bg_rep", [P, E])
        before = sb("before", [P, P], BF16)
        ones = sb("ones", [P, P], BF16)
        w1_sb = sb("w1_sb", [P, E, H])
        w2_sb = sb("w2_sb", [P, E, HK, D])
        minus_half = sb("minus_half", [P, TT])
        kc = sb("kc", [P, CONSTS])
        _, _, base, thresholds, numbers, rows_of, lane, one8 = [
            kc[:, a:b] for a, b in zip(K_AT[:-1], K_AT[1:])]
        zero2 = sb("zero2", [P, 1])

        xin = [sb(f"xin{b}", [P, TT, D]) for b in range(B)]
        hT = [sb(f"hT{b}", [P, T + TAPS - 1]) for b in range(B)]
        uc = [sb(f"uc{b}", [P, HALVES, T]) for b in range(B)]
        sz = [sb(f"sz{b}", [P, HALVES, T]) for b in range(B)]
        Brep = [sb(f"Brep{b}", [P, T]) for b in range(B)]
        Crep = [sb(f"Crep{b}", [P, T]) for b in range(B)]
        dparts = [sb(f"dparts{b}", [96, HALVES * 4, T], BF16) for b in range(B)]
        uparts = [sb(f"uparts{b}", [96, HALVES * 4, T], BF16) for b in range(B)]
        state = sb("state", [P, B, HALVES, 4, 4])
        bst = sb("bst", [P, TT, 6])
        mv = sb("mv", [P, TT, 2])
        veps = sb("veps", [P, TT])
        rstd = sb("rstd", [P, TT])
        xdbl = sb("xdbl", [RANK + 2 * N, T])
        pre = sb("pre", [P, 4, T])
        t1, t2 = pre[:, 0:2, :], pre[:, 2:4, :]
        t3 = sb("t3", [P, HALVES, T])
        xhat = sb("xhat", [P, TT, D])
        t4 = sb("t4", [P, HALVES, T])
        dpart = [sb(f"dpart{p}", [P, HALVES, T], BF16) for p in range(3)]
        upart = [sb(f"upart{p}", [P, HALVES, T], BF16) for p in range(3)]
        decay = sb("decay", [P, 4, T])
        inflow = sb("inflow", [P, 2, T])
        hs = sb("hs", [P, 2, 4, T])
        hc = sb("hc", [P, 2, 4, T])
        scratch = hs[:].rearrange("p a j t -> p (a j t)")
        win_raw = scratch[:, 0:512].rearrange("p (c d) -> p c d", c=4)
        wtap_raw = scratch[:, 512:1536].rearrange("p (h k d) -> p h k d", h=HALVES, k=TAPS)
        wxp_raw = scratch[0:RANK + 2 * N, 1536:1792]
        wdt_raw = scratch[:, 1792:1920].rearrange("p (h r) -> p h r", h=HALVES)
        wout_raw = scratch[:, 1920:2176]
        alog_raw = scratch[0:DI * N // P, 2176:2304]
        yg = sb("yg", [P, HALVES, T])
        xres = sb("xres", [P, TT, D])
        res = sb("res", [P, TT, D])
        cst = sb("cst", [P, TT, 6])
        cmv = sb("cmv", [P, TT, 2])
        cveps = sb("cveps", [P, TT])
        crstd = sb("crstd", [P, TT])
        xn = sb("xn", [P, TT, D])
        xnT = sb("xnT", [P, T])
        lg = sb("lg", [P, TT, E])
        carrier = sb("carrier", [P, 10])
        top = sb("top", [P, TT, 8])
        topi = sb("topi", [P, TT, 8], U32)
        topf = sb("topf", [P, TT, 2])
        oh = sb("oh", [P, TT, 2, E])
        taken = sb("taken", [P, TT, E], BF16)
        ex = sb("ex", [P, TT, E])
        esum = sb("esum", [P, TT])
        erec = sb("erec", [P, TT])
        probs = sb("probs", [P, UNITS * TT * 2])
        rank = sb("rank", [P, TT, E])
        masked = sb("masked", [P, TT, 2, E])
        run = sb("run", [P, E])
        posf = sb("posf", [P, TT, 2])
        ids = [sb(f"ids{b}", [P, TT, 2]) for b in range(B)]
        pos = [sb(f"pos{b}", [P, TT * 2], U32) for b in range(B)]
        count = sb("count", [P, E])
        plan_room = decay[:].rearrange("p a t -> p (a t)")
        over = plan_room[:, 0:E * NTOK // P].rearrange("p (e n) -> p e n", e=E)
        tiles = sb("tiles", [P, E])
        cum = sb("cum", [P, E])
        past = plan_room[:, 256:256 + MAXT * E].rearrange("p (j e) -> p j e", e=E)
        pastc = plan_room[:, 1024:1024 + MAXT * E].rearrange("p (j e) -> p j e", e=E)
        region = sb("region", [P, MAXT])
        start = sb("start", [P, MAXT])
        expert = sb("expert", [P, MAXT])
        etab = sb("etab", [P, MAXT], U32)
        within = sb("within", [P, MAXT])
        lrow = sb("lrow", [P, MAXT])
        pick = sb("pick", [P, 3, MAXT])
        lists = sb("lists", [P, 3, P])
        dstf = sb("dstf", [P, MAXT])
        srcf = sb("srcf", [P, MAXT])
        fix1 = sb("fix1", [P, MAXT])
        fix2 = sb("fix2", [P, MAXT])
        dst_tab = sb("dst_tab", [P, MAXT], U32)
        src_tab = sb("src_tab", [P, MAXT], U32)
        src_now = sb("src_now", [P, 4], U32)
        dst_now = sb("dst_now", [P, 4], U32)
        b1_rep = hs[:].rearrange("p a j t -> p (a j t)")
        free = hc[:].rearrange("p a j t -> p (a j t)")
        b2_rep = free[:, 0:1024]
        hbuf = free[:, 1024:2048].rearrange("p (a h) -> p a h", a=2)
        hTs = free[:, 2048:3072].rearrange("p (a h) -> p a h", a=2)
        xg = free[:, 3072:3584].rearrange("p (a d) -> p a d", a=4)
        xTs = free[:, 3584:3840].rearrange("p (a d) -> p a d", a=2)
        ybuf = sb("ybuf", [P, 4, D])
        ycomb = decay[:].rearrange("p (b k) (t d) -> p b k t d", b=2, t=TT)
        xcomb = pre[:, 0:2, :].rearrange("p b (t d) -> p b t d", t=TT)
        total = t3[:].rearrange("p b (t d) -> p b t d", t=TT)
        final = t4[:].rearrange("p b (t d) -> p b t d", t=TT)
        pcur = sb("pcur", [P, 2, TT, 2])
        fst = sb("fst", [P, TT, 6])
        fmv = [sb(f"fmv{b}", [P, TT, 2]) for b in range(2)]
        fveps = [sb(f"fveps{b}", [P, TT]) for b in range(2)]
        frstd = [sb(f"frstd{b}", [P, TT]) for b in range(2)]

        bank = [ctx.enter_context(nc.psum_tensor(f"bank{i}", [P, 512], F32)) for i in range(8)]
        drep, urep, ybank, fbanks, mbank = bank[0:2], bank[2:4], bank[4], bank[5:7], bank[7]
        xT_banks, h_banks, hT_banks, o_banks = (bank[0], bank[7]), bank[1:3], bank[3:5], bank[5:7]

        s_w = sem("weights_loaded")
        s_w2 = sem("gate_weights_and_constants_loaded")
        s_w3 = sem("expert_weights_loaded")
        s_k = sem("pool_constants")
        s_tap = sem("taps_scaled")
        s_pT = sem("weights_transposed")
        s_pe = sem("weights_evacuated")
        s_negA = sem("negA_done")
        s_zero = sem("dve_constants")
        s_x = [sem(f"x_loaded{b}") for b in range(B)]
        s_dstack = [sem(f"delta_parts_stacked{b}") for b in range(B)]
        s_ustack = [sem(f"du_parts_stacked{b}") for b in range(B)]
        s_rep = [sem(f"bc_loaded{b}") for b in range(B)]
        s_xr = sem("xres_loaded")
        s_sp = sem("sync_steps")
        s_out = [sem(f"out_stored{b}") for b in range(B)]
        s_spill = sem("xn_spilled")
        s_list = sem("list_filled_with_spare_rows")
        s_zres = sem("results_zeroed")
        s_pos = sem("list_places")
        s_scat = [sem(f"rows_listed{b}") for b in range(B)]
        s_plan = sem("plan_steps")
        s_lists = sem("lists_loaded")
        s_pick = sem("rows_picked")
        s_bias = sem("biases_loaded")
        e_si = sem("source_index")
        e_cg = sem("gather_carrier")
        e_cs = sem("scatter_carrier")
        e_g = [sem(f"rows_gathered{r}") for r in range(4)]
        e_xT = sem("x_transposed")
        e_xe = sem("x_evacuated")
        e_h = sem("hidden_product")
        e_hb = sem("hidden_biased")
        e_hT = sem("hidden_transposed")
        e_ge = sem("gelu_done")
        e_o = sem("output_product")
        e_ob = sem("output_biased")
        e_di = sem("destination_index")
        e_sc = [sem(f"results_scattered{r}") for r in range(4)]
        c_in = [sem(f"sum_operands_loaded{b}") for b in range(2)]
        c_p = sem("probs_copied")
        c_1 = sem("first_added")
        c_2 = sem("second_added")
        s_fst = sem("front_stats")
        s_fag = sem("front_aggr")
        s_fve = sem("front_veps")
        s_frs = sem("front_rstd")
        s_xh = sem("xhat_done")
        s_ff = sem("front_bank_filled")
        s_fd = sem("front_bank_drained")
        s_carry = sem("conv_carry")
        s_silu = sem("silu_done")
        s_abs = sem("abs_relu_done")
        s_e = sem("e_done")
        s_1pe = sem("one_plus_e")
        s_ln = sem("ln_done")
        s_nc = sem("minus_correction")
        s_l1p = sem("log1p_done")
        s_delta = sem("delta_done")
        s_du = sem("du_done")
        s_hi = sem("hi_parts")
        s_r1 = sem("rest1")
        s_mid = sem("mid_parts")
        s_lo = sem("lo_part_du")
        s_lod = sem("lo_part_delta")
        s_dr = sem("delta_rep_filled")
        s_ur = sem("du_rep_filled")
        s_ex = sem("decay_done")
        s_bu = sem("inflow_done")
        s_sc = sem("scan_done")
        s_st = sem("state_kept")
        s_hc = sem("hc_done")
        s_y = sem("y_added")
        s_yd = sem("y_gated")
        s_mf = sem("m_bank_filled")
        s_md = sem("m_bank_drained")
        s_res = sem("residual_done")
        s_cst = sem("ln1_stats")
        s_cag = sem("ln1_aggr")
        s_cve = sem("ln1_veps")
        s_crs = sem("ln1_rstd")
        s_xn = sem("xn_done")
        s_gate = sem("gate_steps")
        s_oh = sem("one_hots_done")
        s_gex = sem("gate_exp")
        s_fs2 = sem("ln2_stats")
        s_fa2 = sem("ln2_aggr")
        s_fv2 = sem("ln2_veps")
        s_fr2 = sem("ln2_rstd")
        s_fin = sem("fin_done")

        GATE = 13
        MUSES = ["oproj", "xnT", "logits", "rank"]

        def tile_of(q, j):
            return 16 * (q // 4) + 4 * j + q % 4

        AHEAD = 12

        def tile_steps(eng, step):
            for n in range(AHEAD):
                step(Tile(None, n), lambda lag, n=n: n >= lag)
            with eng.Fori(0, (MAXT - AHEAD) // 4) as i:
                for k in range(4):
                    step(Tile(i, AHEAD + k), lambda lag: True)
            for n in range(MAXT, MAXT + 7):
                step(Tile(None, n), lambda lag, n=n: n - lag < MAXT)

        block = ctx.enter_context(nc.Block())

        @block.sync
        def _(sp):
            def passed(semaphore, value):
                after(sp, semaphore, value)
                sp.sem_inc(s_sp, 1)

            def load_x(u):
                passed(s_xh, u.value(1, -1))
                sp.dma_start(xin[u.b][:], x.rearrange("b l d -> (b l) d")[bass.ds(u.chunk() * T + u.b * L, T), :]
                             .rearrange("(t p) d -> p t d", p=P)).then_inc(s_x[u.b], 16)

            def load_xres(u):
                passed(s_res, u.value(1, 0))
                sp.dma_start(xres[:], x[u.b, bass.ds(u.chunk() * T, T), :].rearrange("(t p) d -> p t d", p=P))\
                    .then_inc(s_xr, 16)

            def replicate_bc(u):
                passed(s_fd, u.value(8, 6))
                after(sp, s_hc, u.value(8, -8))
                for i in range(CH):
                    sp.dma_start(Brep[u.b][N * i:N * i + N, :], xdbl[RANK:RANK + N, :]).then_inc(s_rep[u.b], 16)
                    sp.dma_start(Crep[u.b][N * i:N * i + N, :], xdbl[RANK + N:, :]).then_inc(s_rep[u.b], 16)

            def stack_part(u, ready, n, p):
                sp.wait_ge(ready, u.value(2, n + 1))
                part, dst, stacked = ((dpart, dparts, s_dstack), (upart, uparts, s_ustack))[n]
                for j in range(4):
                    sp.dma_start(dst[u.b][32 * p:32 * p + 32, j:j + 5:4, :],
                                 part[p][32 * j:32 * j + 32, :, :]).then_inc(stacked[u.b], 16)

            def stack_parts(u):
                for p, ready in enumerate((s_hi, s_mid)):
                    for n in range(2):
                        stack_part(u, ready, n, p)
                stack_part(u, s_lod, 0, 2)
                stack_part(u, s_lo, 1, 2)

            def spill_xn(u):
                passed(s_xn, u.value(1, 1))
                row = T * u.k if u.i is None else u.i * (2 * T) + T * u.k
                sp.dma_start(spill[bass.ds(row, T), :].rearrange("(t p) d -> p t d", p=P),
                             xn[:]).then_inc(s_spill, 16)

            first, last = Unit(None, 0), Unit(None, UNITS - 1)
            for b in range(B):
                sp.dma_start(xin[b][:], x[b, 0:T, :].rearrange("(t p) d -> p t d", p=P)).then_inc(s_x[b], 16)
            few = nc.allow_non_contiguous_dma(reason="a few hundred elements")
            few.__enter__()
            sp.dma_start(win_raw, in_proj_w.rearrange("(c p) d -> p c d", p=P)).then_inc(s_w, 16)
            sp.dma_start(cw[:], conv_w.rearrange("(h p) a k -> p h (a k)", p=P)).then_inc(s_w, 16)
            sp.dma_start(wxp_raw, x_proj_w).then_inc(s_w, 16)
            sp.dma_start(wdt_raw, dt_proj_w.rearrange("(h p) r -> p h r", p=P)).then_inc(s_w, 16)
            sp.dma_start(wout_raw, out_proj_w).then_inc(s_w, 16)
            sp.dma_start(alog_raw, A_log.rearrange("(g i) n -> g (i n)", i=CH)).then_inc(s_w, 16)
            for dst, src in ((gam, ln_gamma), (bet, ln_beta)):
                sp.dma_start(dst[:], src.unsqueeze(1)).then_inc(s_w, 16)
            for dst, src in ((cb, conv_b), (dtb, dt_proj_b), (dsk, Dskip)):
                sp.dma_start(dst[:], src.rearrange("(h p) -> p h", p=P)).then_inc(s_w, 16)
            sp.dma_start(kc[:], consts).then_inc(s_w2, 16)
            sp.dma_start(row_list.rearrange("(c p) a -> c (p a)", p=P), spare_rows).then_inc(s_list, 16)
            sp.dma_start(wg_sb[:], Wg).then_inc(s_w2, 16)
            sp.dma_start(bg_rep[:], bg.partition_broadcast(P)).then_inc(s_w2, 16)
            few.__exit__(None, None, None)
            sp.wait_ge(s_k, 1)
            zeroed = results.rearrange("(n p a) d -> n p (a d)", p=P, a=16)
            for n in range(zeroed.shape[0]):
                sp.dma_start(zeroed[n], free[:, 0:16 * D]).then_inc(s_zres, 16)
            replicate_bc(first)
            stack_parts(first)
            sp.dma_start(w1_sb[:], W1.rearrange("e d h -> d e h")).then_inc(s_w3, 16)
            sp.dma_start(w2_sb[:], W2.rearrange("e (k p) d -> p e k d", p=P)).then_inc(s_w3, 16)

            def unit(u, has_prev, has_next):
                if has_next:
                    load_x(u.next().next())
                    replicate_bc(u.next())
                if has_prev:
                    spill_xn(u.prev())
                if has_next:
                    stack_parts(u.next())
                load_xres(u)

            unit(first, False, True)
            with sp.Fori(0, (UNITS - 2) // 2) as i:
                for k in (1, 2):
                    unit(Unit(i, k), True, True)
            unit(last, True, False)
            sp.wait_ge(s_hc, 8 * UNITS)
            sp.wait_ge(s_st, 8 * UNITS)
            sp.dma_start(b1_rep, b1.rearrange("e h -> (e h)").partition_broadcast(P)).then_inc(s_bias, 16)
            sp.wait_ge(s_y, 8 * UNITS)
            sp.dma_start(b2_rep, b2.rearrange("e d -> (e d)").partition_broadcast(P)).then_inc(s_bias, 16)
            spill_xn(last)
            for b in range(B):
                sp.wait_ge(s_scat[b], 64 * UNITS + 16)
            by_row = row_list.rearrange("(c p) a -> c (p a)", p=P)
            for n in range(3):
                c = min(P, LC - P * n)
                sp.dma_start(lists[0:c, n, :], by_row[P * n:P * n + c, :]).then_inc(s_lists, 16)
            sp.wait_ge(s_spill, 16 * UNITS + 16)
            sp.wait_ge(s_lod, 2 * UNITS)

            def rows(u, plus=0):
                return bass.ds(plus + (T * u.k if u.i is None else u.i * (2 * T) + T * u.k), T)

            def load_sum(u):
                s_in = c_in[u.b]
                passed(c_2, u.value(1, -1))
                sp.dma_start(xcomb[:, u.b], spill[rows(u), :].rearrange("(t p) d -> p t d", p=P)).then_inc(s_in, 16)
                if u.i is None and u.k == 0:
                    for s_ring in e_sc:
                        sp.wait_ge(s_ring, 4 * MAXT)
                for k in range(2):
                    sp.dma_start(ycomb[:, u.b, k],
                                 results[rows(u, NTOK * k), :].rearrange("(t p) d -> p t d", p=P)).then_inc(s_in, 16)

            def store(u):
                passed(s_fin, u.value(1, 1))
                sp.dma_start(out[u.b, bass.ds(u.chunk() * T, T), :].rearrange("(t p) d -> p t d", p=P),
                             final[:, u.b]).then_inc(s_out[u.b], 16)

            load_sum(Unit(None, 0))
            load_sum(Unit(None, 1))
            with sp.Fori(0, (UNITS - 2) // 2) as i:
                for k in (1, 2):
                    load_sum(Unit(i, k + 1))
                    store(Unit(i, k - 1))
            store(Unit(None, UNITS - 2))
            store(Unit(None, UNITS - 1))
            for b in range(B):
                sp.wait_ge(s_out[b], 8 * UNITS + 16)

        @block.gpsimd
        def _(pool):
            chain = [0]

            def link(ins):
                chain[0] += 1
                ins.then_inc(s_k, 1)
                pool.wait_ge(s_k, chain[0])

            link(nc.gpsimd.memset(hc[:], 0.0))
            link(nc.gpsimd.memset(ident[:], 0.0))
            link(nc.gpsimd.affine_select(out=ident[:], in_=ident[:], compare_op=ALU.not_equal, fill=1.0, base=0,
                                         pattern=[[-1, P]], channel_multiplier=1))
            link(nc.gpsimd.memset(sel[:], 0.0))
            for p in range(3):
                part = sel[32 * p:32 * p + 32, :, :].rearrange("r m (i n) -> r m i n", i=CH)
                link(nc.gpsimd.affine_select(out=part, in_=part, compare_op=ALU.not_equal, fill=1.0, base=0,
                                             pattern=[[-CH, 4], [-1, CH], [0, N]], channel_multiplier=1))
            link(nc.gpsimd.memset(fold[:], 0.0))
            blocks = fold[:].rearrange("p (m c) -> p m c", c=40)[:, :, 0:CH]
            link(nc.gpsimd.memset(blocks, 1.0))
            link(nc.gpsimd.affine_select(out=blocks, in_=blocks, compare_op=ALU.is_ge, fill=0.0, base=0,
                                         pattern=[[0, 4], [-N, CH]], channel_multiplier=1))
            link(nc.gpsimd.affine_select(out=blocks, in_=blocks, compare_op=ALU.is_ge, fill=0.0, base=N - 1,
                                         pattern=[[0, 4], [N, CH]], channel_multiplier=-1))
            link(nc.gpsimd.memset(minus_half[:], -0.5))
            link(nc.gpsimd.memset(ones[:], 1.0))
            link(nc.gpsimd.memset(before[:], 1.0))
            link(nc.gpsimd.affine_select(out=before[:], in_=before[:], compare_op=ALU.is_gt, fill=0.0, base=0,
                                         pattern=[[1, P]], channel_multiplier=-1))

            def power(out_, in_, ready, value, done):
                pool.wait_ge(ready, value)
                nc.gpsimd.tensor_tensor(out_, in_, minus_half[:], ALU.pow).then_inc(done, 1)

            def times_c(u, q):
                pool.wait_ge(s_sc, u.value(32, 4 * q + 4))
                after(pool, s_y, u.value(8, q - 1))
                if q == 0:
                    pool.wait_ge(s_rep[u.b], u.chunk(1) * 256)
                nc.gpsimd.tensor_tensor(hc[:, q % 2], hs[:, q % 2],
                                        Crep[u.b][:].unsqueeze(1).broadcast_to([P, 4, T]),
                                        ALU.mult).then_inc(s_hc, 1)

            def low_du(u):
                pool.wait_ge(s_r1, u.value(2, 2))
                pool.wait_ge(s_mid, u.value(2, 2))
                nc.gpsimd.tensor_tensor(upart[2][:], t2[:], upart[1][:], ALU.subtract).then_inc(s_lo, 2)

            def carry(n):
                return nc.gpsimd.tensor_tensor(carrier[:, n:n + 1], minus_half[:, 0:1], minus_half[:, 0:1], ALU.mult)

            def list_rows(u, t):
                if t == 0:
                    pool.wait_ge(s_pos, u.value(1, 1))
                    carry(8 + u.b)
                for k in range(2):
                    n = 2 * t + k
                    nc.gpsimd.indirect_dma_start(
                        out=row_list, out_offset=bass.IndirectOffsetOnAxis(ap=pos[u.b][:, n:n + 1], axis=0),
                        in_=ids[u.b][:, t, k:k + 1], in_offset=None).then_inc(s_scat[u.b], 16)

            def unit(u, has_prev, has_next):
                for q in range(QUADS):
                    if has_prev:
                        if q == 2:
                            power(crstd[:], cveps[:], s_cve, u.value(1, 0), s_crs)
                    if q == 2 and has_next:
                        power(rstd[:], veps[:], s_fve, u.value(1, 3), s_frs)
                    if q == 6 and has_next:
                        low_du(u.next())
                    if q >= 6 and has_prev:
                        list_rows(u.prev(), q - 6)
                    times_c(u, q)
                if has_prev:
                    for t in (2, 3):
                        list_rows(u.prev(), t)

            first, last = Unit(None, 0), Unit(None, UNITS - 1)
            for b in range(B):
                nc.gpsimd.dma_start(ids[b][:].rearrange("p t k -> p (t k)"), consts[:, K_AT[b]:K_AT[b + 1]])\
                    .then_inc(s_scat[b], 16)
            for n in (1, 2):
                power(rstd[:], veps[:], s_fve, n, s_frs)
            low_du(first)
            pool.wait_ge(s_list, 16)
            pool.wait_ge(s_zres, 16 * (ROWS // (16 * P)))
            unit(first, False, True)
            with pool.Fori(0, (UNITS - 2) // 2) as i:
                for k in (1, 2):
                    unit(Unit(i, k), True, True)
            unit(last, True, False)
            power(crstd[:], cveps[:], s_cve, UNITS, s_crs)
            for t in range(TT):
                list_rows(last, t)

            def gather(t):
                pool.wait_ge(e_si, t.value(1))
                after(pool, e_xT, t.value(-3))
                after(pool, e_cg, t.value(-3))
                carry(t.ring).then_inc(e_cg, 1)
                nc.gpsimd.indirect_dma_start(
                    out=xg[:, t.ring, :], out_offset=None, in_=spill,
                    in_offset=bass.IndirectOffsetOnAxis(ap=src_now[:, t.ring:t.ring + 1], axis=0)).then_inc(e_g[t.ring], 16)

            def scatter(t):
                pool.wait_ge(e_ob, t.value(1))
                pool.wait_ge(e_di, t.value(1))
                after(pool, e_cs, t.value(-3))
                carry(4 + t.ring).then_inc(e_cs, 1)
                nc.gpsimd.indirect_dma_start(
                    out=results, out_offset=bass.IndirectOffsetOnAxis(ap=dst_now[:, t.ring:t.ring + 1], axis=0),
                    in_=ybuf[:, t.ring, :], in_offset=None).then_inc(e_sc[t.ring], 16)

            def step(n, runs):
                if runs(0):
                    gather(n)
                if runs(7):
                    scatter(n.back(7))

            pool.wait_ge(s_spill, 16 * UNITS + 16)
            pool.wait_ge(s_y, 8 * UNITS)
            tile_steps(pool, step)
            power(frstd[0][:], fveps[0][:], s_fv2, 1, s_fr2)
            with pool.Fori(0, (UNITS - 2) // 2) as i:
                for k in (1, 2):
                    power(frstd[k % 2][:], fveps[k % 2][:], s_fv2, Unit(i, k).value(1, 1), s_fr2)
            power(frstd[1][:], fveps[1][:], s_fv2, UNITS, s_fr2)

        @block.tensor
        def _(pe):
            pe.wait_ge(s_k, 3)
            pe.wait_ge(s_tap, 8)
            for h in range(HALVES):
                for k in range(TAPS):
                    nc.tensor.transpose(bank[h][:, P * k:P * k + P], wtap_raw[:, h, k, :], ident[:])
            for h in range(HALVES):
                nc.tensor.transpose(bank[2][:, P * h:P * h + P], win_raw[:, 2 + h, :], ident[:])
                nc.tensor.transpose(bank[2][:, P * (2 + h):P * (3 + h)], wout_raw[:, P * h:P * h + P], ident[:])
            for h in range(HALVES):
                nc.tensor.transpose(bank[3][:, 96 * h:96 * h + 96], wxp_raw[:, P * h:P * h + P], ident[0:96, 0:96])
                nc.tensor.transpose(bank[3][0:RANK, 256 + P * h:256 + P * h + P], wdt_raw[:, h, :], ident[:])
            nc.tensor.transpose(bank[4][:, 0:32], alog_raw, ident[0:32, 0:32]).then_inc(s_pT, 1)
            pe.wait_ge(s_pe, 7)
            pe.wait_ge(s_k, 14)

            def front_bank(u, use):
                after(pe, s_fd, u.value(8, use - 1))
                return fbanks[use % 2]

            def xhat_T(u):
                o = front_bank(u, 0)
                pe.wait_ge(s_xh, u.value(1, 1))
                for t in range(TT):
                    ins = nc.tensor.transpose(o[:, P * t:P * t + P], xhat[:, t, :], ident[:])
                ins.then_inc(s_ff, 1)

            def conv_u(u, h, taps):
                o = fbanks[(1 + h) % 2]
                if 0 in taps:
                    front_bank(u, 1 + h)
                    pe.wait_ge(s_fd, u.value(8, 1))
                for k in taps:
                    ins = nc.tensor.matmul(o[:], wtapT[:, h, k, :], hT[u.b][:, k:k + T],
                                           start=(k == 0), stop=(k == TAPS - 1))
                if TAPS - 1 in taps:
                    ins.then_inc(s_ff, 1)

            def proj_z(u, h):
                o = front_bank(u, 3 + h)
                nc.tensor.matmul(o[:], wzT[:, h, :], hT[u.b][:, TAPS - 1:]).then_inc(s_ff, 1)

            def proj_x(u):
                o = front_bank(u, 5)
                pe.wait_ge(s_silu, u.value(2, 2))
                for h in range(HALVES):
                    ins = nc.tensor.matmul(o[0:96, :], wxpT[:, h, :], uc[u.b][:, h, :], start=(h == 0), stop=(h == 1))
                ins.then_inc(s_ff, 1)

            def proj_dt(u, h):
                o = front_bank(u, 6 + h)
                pe.wait_ge(s_fd, u.value(8, 6))
                nc.tensor.matmul(o[:], wdtT[:, h, :], xdbl[0:RANK, :]).then_inc(s_ff, 1)

            def replicate_delta(u, g):
                if g == 0:
                    pe.wait_ge(s_dstack[u.b], u.chunk(1) * 192)
                after(pe, s_ex, u.value(32, g - 1))
                nc.tensor.matmul(drep[g % 2][:], sel[:, g // 4 % 4, :], dparts[u.b][:, 4 * (g // 16) + g % 4, :])\
                    .then_inc(s_dr, 1)

            def replicate_du(u, g):
                if g == 0:
                    pe.wait_ge(s_ustack[u.b], u.chunk(1) * 192)
                after(pe, s_bu, u.value(32, g - 1))
                nc.tensor.matmul(urep[g % 2][:], sel[:, g // 4 % 4, :], uparts[u.b][:, 4 * (g // 16) + g % 4, :])\
                    .then_inc(s_ur, 1)

            def add_states(u, q, tiles):
                m = q % 4
                if 0 in tiles:
                    pe.wait_ge(s_hc, u.value(8, q + 1))
                    if m == 0:
                        after(pe, s_yd, u.value(2, q // 4))
                for j in tiles:
                    ins = nc.tensor.matmul(ybank[32 * j:32 * j + 32, :], fold[:, 32 * m:32 * m + 32], hc[:, q % 2, j, :],
                                           start=(m == 0), stop=(m == 3))
                if 3 in tiles:
                    ins.then_inc(s_y, 1)

            def add_skip(u, h):
                nc.tensor.matmul(ybank[:], skip[:, h, :], uc[u.b][:, h, :], start=False, stop=False)

            def m_bank(u, use):
                pe.wait_ge(s_md, u.value(4, MUSES.index(use) + 1))
                return mbank

            def out_proj(u, ts):
                if 0 in ts:
                    m_bank(u, "oproj")
                    pe.wait_ge(s_yd, u.value(2, 2))
                for t in ts:
                    for h in range(HALVES):
                        ins = nc.tensor.matmul(mbank[:, P * t:P * t + P], yg[:, h, P * t:P * t + P], woutT[:, h, :],
                                               start=(h == 0), stop=(h == 1))
                if TT - 1 in ts:
                    ins.then_inc(s_mf, 1)

            def xn_T(u):
                o = m_bank(u, "xnT")
                pe.wait_ge(s_xn, u.value(1, 1))
                for t in range(TT):
                    ins = nc.tensor.transpose(o[:, P * t:P * t + P], xn[:, t, :], ident[:])
                ins.then_inc(s_mf, 1)

            def logits(u):
                o = m_bank(u, "logits")
                for t in range(TT):
                    ins = nc.tensor.matmul(o[:, E * t:E * t + E], xnT[:, P * t:P * t + P], wg_sb[:])
                ins.then_inc(s_mf, 1)

            def ranks(u):
                o = m_bank(u, "rank")
                pe.wait_ge(s_gate, u.value(GATE, 5))
                for t in range(TT + 1):
                    oo = o[:, E * t:E * t + E]
                    for s in range(t):
                        ins = nc.tensor.matmul(oo, ones[:], taken[:, s, :], start=(s == 0), stop=(t == TT and s == TT - 1))
                    if t < TT:
                        nc.tensor.matmul(oo, before[:], taken[:, t, :], start=(t == 0), stop=True)
                ins.then_inc(s_mf, 1)

            def states_at(g):
                q, n = (g - 9) // 4, (g - 9) % 4
                if q % 4 == 3:
                    return q, ((0, 1), (2, 3), (), ())[n]
                return q, (n,)

            ahead2 = {18: xhat_T, 21: lambda u: conv_u(u, 0, (0, 1)), 22: lambda u: conv_u(u, 0, (2, 3)),
                      23: lambda u: conv_u(u, 1, (0, 1)), 24: lambda u: conv_u(u, 1, (2, 3))}
            front = {2: lambda u: proj_z(u, 0), 3: lambda u: proj_z(u, 1), 12: proj_x,
                     14: lambda u: proj_dt(u, 0), 15: lambda u: proj_dt(u, 1)}
            back = {10: lambda u: out_proj(u, (0, 1)), 11: lambda u: out_proj(u, (2, 3)),
                    16: xn_T, 18: logits, 21: ranks}

            own = {13: lambda u: add_skip(u, 0), 29: lambda u: add_skip(u, 1)}

            def unit(u, has_prev, has_next):
                replicate_delta(u, 0)
                replicate_delta(u, 1)
                for g in range(4 * QUADS):
                    replicate_du(u, g)
                    if g + 2 < 4 * QUADS:
                        replicate_delta(u, g + 2)
                    if g >= 9:
                        add_states(u, *states_at(g))
                    elif has_prev:
                        q, tiles = states_at(g + 32)
                        add_states(u.prev(), q, tiles)
                    if g in own:
                        own[g](u)
                    if has_next and g in front:
                        front[g](u.next())
                    if has_next and g in ahead2:
                        ahead2[g](u.next().next())
                    if has_prev and g in back:
                        back[g](u.prev())

            first, last = Unit(None, 0), Unit(None, UNITS - 1)
            for u in (first, first.next()):
                for g in sorted(ahead2):
                    ahead2[g](u)
                if u is first:
                    for g in sorted(front):
                        front[g](u)
            pe.wait_ge(s_w2, 48)
            pe.wait_ge(s_negA, 1)
            unit(first, False, True)
            with pe.Fori(0, (UNITS - 2) // 2) as i:
                for k in (1, 2):
                    unit(Unit(i, k), True, True)
            unit(last, True, False)
            for g in range(9):
                q, tiles = states_at(g + 32)
                add_states(last, q, tiles)
            for g in sorted(back):
                back[g](last)

            pe.wait_ge(s_lists, 48)
            pe.wait_ge(s_plan, 12)
            for n in range(3):
                c = min(P, LC - P * n)
                ins = nc.tensor.matmul(mbank[:, 0:MAXT], lists[0:c, n, :], pick[0:c, n, :], start=(n == 0), stop=(n == 2))
            ins.then_inc(s_pick, 1)

            def x_T(t):
                pe.wait_ge(e_g[t.ring], t.dmas(1))
                after(pe, e_xe, t.value(-1))
                nc.tensor.transpose(xT_banks[t.ring % 2][:, 0:P], xg[:, t.ring, :], ident[:]).then_inc(e_xT, 1)

            def hidden(t, e):
                pe.wait_ge(e_xe, t.value(1))
                after(pe, e_hb, t.value(-1))
                nc.tensor.matmul(h_banks[t.ring % 2][:], xTs[:, t.ring % 2, :],
                                 w1_sb[:].rearrange("p e h -> p (e h)")[:, bass.ds(e * H, H)]).then_inc(e_h, 1)

            def hidden_T(t):
                pe.wait_ge(e_hb, t.value(1))
                after(pe, e_ge, t.value(-1))
                for k in range(HK):
                    ins = nc.tensor.transpose(hT_banks[t.ring % 2][:, P * k:P * k + P],
                                              hbuf[:, t.ring % 2, P * k:P * k + P], ident[:])
                ins.then_inc(e_hT, 1)

            def output(t, e):
                pe.wait_ge(e_ge, t.value(1))
                after(pe, e_ob, t.value(-1))
                for k in range(HK):
                    ins = nc.tensor.matmul(o_banks[t.ring % 2][:, 0:D], hTs[:, t.ring % 2, P * k:P * k + P],
                                           w2_sb[:].rearrange("p e k d -> p (e k d)")[:, bass.ds(e * (HK * D) + k * D, D)],
                                           start=(k == 0), stop=(k == HK - 1))
                ins.then_inc(e_o, 1)

            def expert_of(t):
                return pe.value_load(etab[0:1, t.at()], min_val=0, max_val=E - 1)

            known = {}

            def step(n, runs):
                if n.i is not None and n.k == AHEAD:
                    known.clear()
                if n.i is None and n.k >= MAXT:
                    known.clear()
                if runs(4):
                    known[n.k - 4] = expert_of(n.back(4))
                e_h_now = known.get(n.k - 4)
                if runs(6) and n.k - 6 not in known:
                    known[n.k - 6] = expert_of(n.back(6))
                e_o_now = known.get(n.k - 6)
                if runs(3):
                    x_T(n.back(3))
                if runs(4):
                    hidden(n.back(4), e_h_now)
                if runs(5):
                    hidden_T(n.back(5))
                if runs(6):
                    output(n.back(6), e_o_now)

            pe.wait_ge(s_w3, 32)
            tile_steps(pe, step)

        @block.scalar
        def _(act):
            act.wait_ge(s_pT, 1)
            for h in range(HALVES):
                nc.scalar.copy(wtapT[:, h].rearrange("p k c -> p (k c)"), bank[h][:]).then_inc(s_pe, 1)
            nc.scalar.copy(wzT[:].rearrange("p h c -> p (h c)"), bank[2][:, 0:256]).then_inc(s_pe, 1)
            nc.scalar.copy(woutT[:].rearrange("p h c -> p (h c)"), bank[2][:, 256:512]).then_inc(s_pe, 1)
            nc.scalar.copy(wxpT[:].rearrange("p h c -> p (h c)"), bank[3][:, 0:192]).then_inc(s_pe, 1)
            nc.scalar.copy(wdtT[:].rearrange("p h c -> p (h c)"), bank[3][0:RANK, 256:512]).then_inc(s_pe, 1)
            nc.scalar.activation(aexp[:], bank[4][:, 0:32], ACT.Exp).then_inc(s_pe, 1)

            def filled(u, use):
                act.wait_ge(s_ff, u.value(8, use + 1))

            def h_evac(u):
                nc.scalar.copy(hT[u.b][:, 0:TAPS - 1], hT[u.b][:, T:]).then_inc(s_carry, 1)
                act.wait_ge(s_carry, u.value(1, 1))
                filled(u, 0)
                nc.scalar.activation(hT[u.b][:, TAPS - 1:], fbanks[0][:], ACT.Identity, bias=bet[:], scale=gam[:])\
                    .then_inc(s_fd, 1)

            def u_evac(u, h):
                filled(u, 1 + h)
                after(act, s_lod, u.value(2, 0))
                after(act, s_lo, u.value(2, 0))
                nc.scalar.activation(pre[:, 2 * h, :], fbanks[(1 + h) % 2][:], ACT.Identity, bias=cb[:, h:h + 1]).then_inc(s_fd, 1)

            def z_evac(u, h):
                filled(u, 3 + h)
                nc.scalar.activation(pre[:, 2 * h + 1, :], fbanks[(3 + h) % 2][:], ACT.Copy).then_inc(s_fd, 1)

            def silus(u):
                act.wait_ge(s_fd, u.value(8, 5))
                after(act, s_yd, u.value(2, -2))
                nc.scalar.activation(uc[u.b][:], pre[:, 0:4:2, :], ACT.Silu).then_inc(s_silu, 1)
                nc.scalar.activation(sz[u.b][:], pre[:, 1:4:2, :], ACT.Silu).then_inc(s_silu, 1)

            def xdbl_evac(u):
                filled(u, 5)
                after(act, s_rep[1 - u.b], u.prev().chunk(1) * 256 if (u.i is not None or u.k) else 0)
                nc.scalar.copy(xdbl[:], fbanks[1][0:96, :]).then_inc(s_fd, 1)

            def dt_evac(u, h):
                filled(u, 6 + h)
                o = fbanks[h]
                nc.scalar.activation(t1[:, h, :], o[:], ACT.Abs, bias=dtb[:, h:h + 1]).then_inc(s_abs, 1)
                nc.scalar.activation(t4[:, h, :], o[:], ACT.Relu, bias=dtb[:, h:h + 1]).then_inc(s_fd, 1)

            def exponential(u):
                act.wait_ge(s_abs, u.value(2, 2))
                nc.scalar.activation(t1[:], t1[:], ACT.Exp, scale=-1.0).then_inc(s_e, 1)
                act.wait_ge(s_e, u.value(1, 1))
                nc.scalar.activation(t2[:], t1[:], ACT.Copy, bias=1.0).then_inc(s_1pe, 1)

            def logarithm(u):
                act.wait_ge(s_1pe, u.value(1, 1))
                nc.scalar.activation(t3[:], t2[:], ACT.Ln).then_inc(s_ln, 1)

            def hi_part(u, n):
                after(act, (s_dstack, s_ustack)[n][1 - u.b],
                      u.prev().chunk(1) * 192 if (u.i is not None or u.k) else 0)
                act.wait_ge((s_delta, s_du)[n], u.value(1, 1))
                nc.scalar.copy((dpart, upart)[n][0][:], (t3, t4)[n][:]).then_inc(s_hi, 1)

            def mid_part(u, n):
                act.wait_ge(s_r1, u.value(2, n + 1))
                nc.scalar.copy((dpart, upart)[n][1][:], (t1, t2)[n][:]).then_inc(s_mid, 1)

            def decays(u, g):
                act.wait_ge(s_dr, u.value(32, g + 1))
                after(act, s_sc, u.value(32, g - 3))
                ch = tile_of(g // 4, g % 4)
                nc.scalar.activation(decay[:, g % 4, :], drep[g % 2][:], ACT.Exp, scale=negA[:, ch:ch + 1]).then_inc(s_ex, 1)

            def xnT_evac(u):
                act.wait_ge(s_mf, u.value(4, 2))
                nc.scalar.copy(xnT[:], mbank[:]).then_inc(s_md, 1)

            def gate_exp(u):
                act.wait_ge(s_gate, u.value(GATE, 2))
                nc.scalar.activation(ex[:], ex[:], ACT.Exp).then_inc(s_gex, 1)

            front = {1: lambda u: u_evac(u, 0), 2: lambda u: u_evac(u, 1), 5: lambda u: z_evac(u, 0),
                     6: lambda u: z_evac(u, 1), 11: silus, 15: xdbl_evac, 17: lambda u: dt_evac(u, 0),
                     18: lambda u: (dt_evac(u, 1), exponential(u)), 20: logarithm, 23: lambda u: hi_part(u, 0),
                     24: lambda u: hi_part(u, 1), 26: lambda u: mid_part(u, 0), 27: lambda u: mid_part(u, 1)}
            ahead2 = {20: h_evac}
            back = {18: xnT_evac, 22: gate_exp}

            def unit(u, has_prev, has_next):
                for g in range(4 * QUADS):
                    decays(u, g)
                    if has_next and g in front:
                        front[g](u.next())
                    if has_next and g in ahead2:
                        ahead2[g](u.next().next())
                    if has_prev and g in back:
                        back[g](u.prev())

            first, last = Unit(None, 0), Unit(None, UNITS - 1)
            act.wait_ge(s_zero, 3)
            h_evac(first)
            for g in sorted(front):
                front[g](first)
            h_evac(first.next())
            act.wait_ge(s_negA, 1)
            unit(first, False, True)
            with act.Fori(0, (UNITS - 2) // 2) as i:
                for k in (1, 2):
                    unit(Unit(i, k), True, True)
            unit(last, True, False)
            for g in sorted(back):
                back[g](last)

            def x_evac(t):
                act.wait_ge(e_xT, t.value(1))
                after(act, e_h, t.value(-1))
                nc.scalar.copy(xTs[:, t.ring % 2, :], xT_banks[t.ring % 2][:, 0:P]).then_inc(e_xe, 1)

            def gelu(t):
                act.wait_ge(e_hT, t.value(1))
                after(act, e_o, t.value(-1))
                nc.scalar.activation(hTs[:, t.ring % 2, :], hT_banks[t.ring % 2][:], ACT.Gelu).then_inc(e_ge, 1)

            def step(n, runs):
                if runs(3):
                    x_evac(n.back(3))
                if runs(5):
                    gelu(n.back(5))

            act.wait_ge(s_y, 8 * UNITS)
            tile_steps(act, step)

        @block.vector
        def _(dve):
            nc.vector.memset(state[:], 0.0).then_inc(s_zero, 1)
            for b in range(B):
                nc.vector.memset(hT[b][:, T:], 0.0).then_inc(s_zero, 1)
            dve.wait_ge(s_w, 16 * 11)
            for h in range(HALVES):
                for k in range(TAPS):
                    nc.vector.tensor_scalar(wtap_raw[:, h, k, :], win_raw[:, h, :], cw[:, h, k:k + 1], None,
                                            ALU.mult).then_inc(s_tap, 1)
            dve.wait_ge(s_pe, 7)
            dve.wait_ge(s_k, 3)
            for h in range(HALVES):
                nc.vector.tensor_scalar(skip[:, h, :], ident[:], dsk[:, h:h + 1], None, ALU.mult)
            nc.vector.tensor_scalar(negA[:], aexp[:], -1.0, None, ALU.mult).then_inc(s_negA, 1)

            def moments(u, src, st, mvar, ve, eps, s1, s2, s3):
                for t in range(TT):
                    ins = nc.vector.bn_stats(st[:, t, :], src[:, t, :])
                ins.then_inc(s1, 1)
                dve.wait_ge(s1, u.value(1, 1))
                nc.vector.tensor_copy(zero2[:], zero2[:])
                for t in range(TT):
                    ins = nc.vector.bn_aggr(mvar[:, t, :], st[:, t, :])
                ins.then_inc(s2, 1)
                dve.wait_ge(s2, u.value(1, 1))
                nc.vector.tensor_scalar(ve[:], mvar[:, :, 1], eps, None, ALU.add).then_inc(s3, 1)

            def normalise(u, dst, src, mvar, rs, ready, done):
                dve.wait_ge(ready, u.value(1, 1))
                for t in range(TT):
                    ins = nc.vector.tensor_scalar(dst[:, t, :], src[:, t, :], mvar[:, t, 0:1], rs[:, t:t + 1],
                                                  ALU.subtract, ALU.mult)
                ins.then_inc(done, 1)

            def front_stats(u):
                dve.wait_ge(s_x[u.b], u.chunk(1) * 16)
                moments(u, xin[u.b], bst, mv, veps, 1e-6, s_fst, s_fag, s_fve)

            def front_norm(u):
                after(dve, s_ff, u.value(8, -7))
                normalise(u, xhat, xin[u.b], mv, rstd, s_frs, s_xh)

            def softplus(u):
                dve.wait_ge(s_ln, u.value(1, 1))
                nc.vector.scalar_tensor_tensor(t2[:], t2[:], 1.0, t1[:], ALU.subtract, ALU.subtract).then_inc(s_nc, 1)
                dve.wait_ge(s_nc, u.value(1, 1))
                nc.vector.tensor_tensor(t3[:], t3[:], t2[:], ALU.subtract).then_inc(s_l1p, 1)
                dve.wait_ge(s_l1p, u.value(2, 1))
                nc.vector.tensor_tensor(t3[:], t3[:], t1[:], ALU.min).then_inc(s_l1p, 1)
                dve.wait_ge(s_l1p, u.value(2, 2))
                nc.vector.tensor_tensor(t3[:], t3[:], t4[:], ALU.add).then_inc(s_delta, 1)

            def delta_u(u):
                dve.wait_ge(s_delta, u.value(1, 1))
                nc.vector.tensor_tensor(t4[:], t3[:], uc[u.b][:], ALU.mult).then_inc(s_du, 1)

            def rest(u, n):
                dve.wait_ge(s_hi, u.value(2, n + 1))
                dst, src, part = ((t1, t3, dpart), (t2, t4, upart))[n]
                nc.vector.tensor_tensor(dst[:], src[:], part[0][:], ALU.subtract).then_inc(s_r1, 1)

            def low_delta(u):
                dve.wait_ge(s_r1, u.value(2, 1))
                dve.wait_ge(s_mid, u.value(2, 1))
                nc.vector.tensor_tensor(dpart[2][:], t1[:], dpart[1][:], ALU.subtract).then_inc(s_lod, 2)

            def inflows(u, g):
                dve.wait_ge(s_ur, u.value(32, g + 1))
                if g == 0:
                    dve.wait_ge(s_rep[u.b], u.chunk(1) * 256)
                after(dve, s_sc, u.value(32, g - 1))
                nc.vector.tensor_tensor(inflow[:, g % 2, :], urep[g % 2][:], Brep[u.b][:], ALU.mult).then_inc(s_bu, 1)

            def keep(u, q):
                dve.wait_ge(s_sc, u.value(32, 4 * q + 4))
                nc.vector.tensor_copy(state[:, u.b, q // 4, q % 4, :], hs[:, q % 2, :, T - 1]).then_inc(s_st, 1)

            def scan(u, g):
                q, j = g // 4, g % 4
                dve.wait_ge(s_ex, u.value(32, g + 1))
                dve.wait_ge(s_bu, u.value(32, g + 1))
                if j == 0:
                    after(dve, s_hc, u.value(8, q - 1))
                    after(dve, s_st, u.value(8, q - 1))
                nc.vector.tensor_tensor_scan(hs[:, q % 2, j, :], decay[:, j, :], inflow[:, g % 2, :],
                                             state[:, u.b, q // 4, q % 4, j:j + 1], ALU.mult, ALU.add).then_inc(s_sc, 1)

            def post(u, h):
                dve.wait_ge(s_y, u.value(8, 4 * h + 4))
                nc.vector.tensor_tensor(yg[:, h, :], ybank[:], sz[u.b][:, h, :], ALU.mult).then_inc(s_yd, 1)

            def residual(u):
                dve.wait_ge(s_mf, u.value(4, 1))
                dve.wait_ge(s_xr, u.value(16, 16))
                nc.vector.scalar_tensor_tensor(res[:].rearrange("p t d -> p (t d)"),
                                               xres[:].rearrange("p t d -> p (t d)"), 2.0, mbank[:],
                                               ALU.mult, ALU.add).then_inc(s_md, 1)
                dve.wait_ge(s_md, u.value(4, 2))
                nc.vector.tensor_copy(zero2[:], res[:, 0, 0:1]).then_inc(s_res, 1)
                moments(u, res, cst, cmv, cveps, 1e-5, s_cst, s_cag, s_cve)

            def norm1(u):
                dve.wait_ge(s_spill, u.value(16, 16))
                normalise(u, xn, res, cmv, crstd, s_crs, s_xn)

            def at(u, n):
                return u.value(GATE, n)

            def gate(u):
                dve.wait_ge(s_mf, u.value(4, 3))
                nc.vector.tensor_tensor(lg[:], mbank[:, 0:TT * E].rearrange("p (t e) -> p t e", e=E),
                                        bg_rep[:].unsqueeze(1).broadcast_to([P, TT, E]), ALU.add).then_inc(s_md, 1)
                dve.wait_ge(s_md, u.value(4, 4))
                nc.vector.tensor_copy(zero2[:], zero2[:])
                for t in range(TT):
                    ins = nc.vector.max(top[:, t, :], lg[:, t, :])
                ins.then_inc(s_gate, 1)
                dve.wait_ge(s_gate, at(u, 1))
                nc.vector.tensor_tensor(ex[:], top[:], top[:, :, 0:1].broadcast_to([P, TT, E]),
                                        ALU.subtract).then_inc(s_gate, 1)
                for t in range(TT):
                    ins = nc.vector.max_index(topi[:, t, :], top[:, t, :], lg[:, t, :])
                ins.then_inc(s_gate, 1)
                dve.wait_ge(s_gate, at(u, 3))
                nc.vector.tensor_copy(topf[:], topi[:, :, 0:2]).then_inc(s_gate, 1)
                dve.wait_ge(s_gate, at(u, 4))
                for k in range(2):
                    ins = nc.vector.tensor_tensor(oh[:, :, k, :], lane.unsqueeze(1).broadcast_to([P, TT, E]),
                                                  topf[:, :, k:k + 1].broadcast_to([P, TT, E]), ALU.is_equal)
                ins.then_inc(s_oh, 1)
                dve.wait_ge(s_oh, u.value(1, 1))
                nc.vector.tensor_tensor(taken[:], oh[:, :, 0, :], oh[:, :, 1, :], ALU.add).then_inc(s_gate, 1)

            def place(u):
                dve.wait_ge(s_gex, u.value(1, 1))
                nc.vector.reduce_sum(esum[:], ex[:], AX_X).then_inc(s_gate, 1)
                dve.wait_ge(s_gate, at(u, 6))
                nc.vector.reciprocal(erec[:], esum[:]).then_inc(s_gate, 1)
                dve.wait_ge(s_gate, at(u, 7))
                w = 2 * TT
                here = bass.ds(w * u.k if u.i is None else u.i * (2 * w) + w * u.k, w)
                nc.vector.tensor_tensor(probs[:, here].rearrange("p (t k) -> p t k", k=2), ex[:, :, 0:2],
                                        erec[:].unsqueeze(2).broadcast_to([P, TT, 2]), ALU.mult).then_inc(s_gate, 1)
                dve.wait_ge(s_mf, u.value(4, 4))
                counts = mbank[:, 0:(TT + 1) * E].rearrange("p (t e) -> p t e", e=E)
                nc.vector.tensor_tensor(rank[:], counts[:, 0:TT, :], run[:].unsqueeze(1).broadcast_to([P, TT, E]),
                                        ALU.add).then_inc(s_gate, 1)
                dve.wait_ge(s_gate, at(u, 9))
                nc.vector.tensor_tensor(run[:], run[:], counts[:, TT, :], ALU.add).then_inc(s_md, 1)
                for k in range(2):
                    ins = nc.vector.tensor_tensor(masked[:, :, k, :], oh[:, :, k, :], rank[:], ALU.mult)
                ins.then_inc(s_gate, 1)
                dve.wait_ge(s_gate, at(u, 10))
                nc.vector.reduce_sum(posf[:].rearrange("p t k -> p (t k)"), masked[:].rearrange("p t k e -> p (t k) e"),
                                     AX_X).then_inc(s_gate, 1)
                dve.wait_ge(s_scat[u.b], u.chunk() * 128 + 16)
                nc.vector.tensor_scalar(ids[u.b][:], ids[u.b][:], 2.0 * T, None, ALU.add).then_inc(s_gate, 1)
                dve.wait_ge(s_gate, at(u, 11))
                nc.vector.tensor_copy(pos[u.b][:], posf[:].rearrange("p t k -> p (t k)")).then_inc(s_gate, 1)
                dve.wait_ge(s_gate, at(u, 13))
                dve.sem_inc(s_pos, 1)

            front = {18: softplus, 19: delta_u,
                     21: lambda u: rest(u, 0), 22: lambda u: rest(u, 1), 24: low_delta}
            ahead2 = {7: front_stats, 14: front_norm}
            back = {6: lambda u: post(u, 1), 10: residual, 13: norm1, 17: gate, 23: place}

            def unit(u, has_prev, has_next):
                for g in range(4 * QUADS):
                    if g == 0:
                        inflows(u, 0)
                    if g < 31:
                        inflows(u, g + 1)
                    if g % 4 == 0 and g > 0:
                        keep(u, g // 4 - 1)
                    scan(u, g)
                    if has_next and g in front:
                        front[g](u.next())
                    if has_next and g in ahead2:
                        ahead2[g](u.next().next())
                    if has_prev and g in back:
                        back[g](u.prev())
                    if g == 22:
                        post(u, 0)
                keep(u, QUADS - 1)

            first, last = Unit(None, 0), Unit(None, UNITS - 1)
            nc.vector.memset(zero2[:], 0.0).then_inc(s_zero, 1)
            dve.wait_ge(s_zero, 4)
            dve.sem_inc(s_md, 1)
            dve.sem_inc(s_spill, 16)
            for b in range(B):
                dve.sem_inc(s_out[b], 16)
            front_stats(first)
            front_norm(first)
            front_stats(first.next())
            front_norm(first.next())
            for g in sorted(front):
                front[g](first)
            dve.wait_ge(s_w2, 48)
            nc.vector.tensor_copy(run[:], base).then_inc(s_zero, 1)
            dve.wait_ge(s_zero, 5)
            unit(first, False, True)
            with dve.Fori(0, (UNITS - 2) // 2) as i:
                for k in (1, 2):
                    unit(Unit(i, k), True, True)
            unit(last, True, False)
            for g in sorted(back):
                back[g](last)

            planned = [0]

            def plan(ins):
                planned[0] += 1
                ins.then_inc(s_plan, 1)
                dve.wait_ge(s_plan, planned[0])

            dve.wait_ge(s_md, 4 * UNITS + 1)
            plan(nc.vector.tensor_tensor(count[:], run[:], base, ALU.subtract))
            plan(nc.vector.tensor_tensor(over, count[:].unsqueeze(2).broadcast_to([P, E, NTOK // P]),
                                         thresholds.unsqueeze(1).broadcast_to([P, E, NTOK // P]), ALU.is_gt))
            plan(nc.vector.reduce_sum(tiles[:], over, AX_X))
            plan(nc.vector.tensor_tensor_scan(cum[:], one8, tiles[:],
                                              0.0, ALU.mult, ALU.add))
            cums = cum[:].unsqueeze(1).broadcast_to([P, MAXT, E])
            plan(nc.vector.tensor_tensor(past, numbers.unsqueeze(2).broadcast_to([P, MAXT, E]), cums, ALU.is_ge))
            plan(nc.vector.tensor_tensor(pastc, past, cums, ALU.mult))
            plan(nc.vector.reduce_sum(region[:], past, AX_X))
            plan(nc.vector.reduce_max(start[:], pastc, AX_X))
            plan(nc.vector.tensor_tensor(within[:], numbers, start[:], ALU.subtract))
            plan(nc.vector.scalar_tensor_tensor(lrow[:], region[:], float(NTOK // P), within[:], ALU.mult, ALU.add))
            plan(nc.vector.tensor_scalar(expert[:], region[:], float(E - 1), None, ALU.min))
            for n in range(3):
                ins = nc.vector.tensor_scalar(pick[:, n, :], lrow[:], rows_of[:, n:n + 1], None, ALU.is_equal)
            plan(ins)
            plan(nc.vector.tensor_copy(etab[:], expert[:]))
            dve.wait_ge(s_pick, 1)
            plan(nc.vector.tensor_copy(dstf[:], mbank[:, 0:MAXT]))
            plan(nc.vector.tensor_copy(dst_tab[:], dstf[:]))
            plan(nc.vector.tensor_scalar(fix1[:], dstf[:], float(NTOK), -float(NTOK), ALU.is_ge, ALU.mult))
            plan(nc.vector.tensor_scalar(fix2[:], dstf[:], float(2 * NTOK), -float(NTOK), ALU.is_ge, ALU.mult))
            plan(nc.vector.tensor_tensor(fix1[:], fix1[:], fix2[:], ALU.add))
            plan(nc.vector.tensor_tensor(srcf[:], dstf[:], fix1[:], ALU.add))
            plan(nc.vector.tensor_copy(src_tab[:], srcf[:]))

            def source(t):
                after(dve, e_g[t.ring], t.dmas(0))
                nc.vector.tensor_copy(src_now[:, t.ring:t.ring + 1], src_tab[:, t.at()]).then_inc(e_si, 1)

            def hidden_bias(t):
                e = dve.value_load(etab[0:1, t.at()], min_val=0, max_val=E - 1)
                dve.wait_ge(e_h, t.value(1))
                after(dve, e_hT, t.value(-1))
                nc.vector.tensor_tensor(hbuf[:, t.ring % 2, :], h_banks[t.ring % 2][:], b1_rep[:, bass.ds(e * H, H)],
                                        ALU.add).then_inc(e_hb, 1)

            def output_bias(t):
                e = dve.value_load(etab[0:1, t.at()], min_val=0, max_val=E - 1)
                dve.wait_ge(e_o, t.value(1))
                after(dve, e_sc[t.ring], t.dmas(0))
                nc.vector.tensor_tensor(ybuf[:, t.ring, :], o_banks[t.ring % 2][:, 0:D], b2_rep[:, bass.ds(e * D, D)],
                                        ALU.add).then_inc(e_ob, 1)
                nc.vector.tensor_copy(dst_now[:, t.ring:t.ring + 1], dst_tab[:, t.at()]).then_inc(e_di, 1)

            def step(n, runs):
                if runs(0):
                    source(n)
                if runs(4):
                    hidden_bias(n.back(4))
                if runs(6):
                    output_bias(n.back(6))

            dve.wait_ge(s_bias, 32)
            tile_steps(dve, step)

            def add_experts(u):
                w = 2 * TT
                here = bass.ds(w * u.k if u.i is None else u.i * (2 * w) + w * u.k, w)
                nc.vector.tensor_copy(pcur[:, u.b].rearrange("p t k -> p (t k)"), probs[:, here]).then_inc(c_p, 1)
                dve.wait_ge(c_p, u.value(1, 1))
                dve.wait_ge(c_in[u.b], u.chunk(1) * 48)
                for k in range(2):
                    for t in range(TT):
                        ins = nc.vector.scalar_tensor_tensor(
                            total[:, u.b, t, :], ycomb[:, u.b, k, t, :], pcur[:, u.b, t, k:k + 1],
                            xcomb[:, u.b, t, :] if k == 0 else total[:, u.b, t, :], ALU.mult, ALU.add)
                    ins.then_inc((c_1, c_2)[k], 1)
                    dve.wait_ge((c_1, c_2)[k], u.value(1, 1))
                moments(u, total[:, u.b], fst, fmv[u.b], fveps[u.b], 1e-5, s_fs2, s_fa2, s_fv2)

            def norm2(u):
                dve.wait_ge(s_out[u.b], u.chunk() * 16 + 16)
                normalise(u, final[:, u.b], total[:, u.b], fmv[u.b], frstd[u.b], s_fr2, s_fin)

            add_experts(Unit(None, 0))
            with dve.Fori(0, (UNITS - 2) // 2) as i:
                for k in (1, 2):
                    add_experts(Unit(i, k))
                    norm2(Unit(i, k - 1))
            add_experts(Unit(None, UNITS - 1))
            norm2(Unit(None, UNITS - 2))
            norm2(Unit(None, UNITS - 1))


_INS = ["L0_attn_x", "L0_attn_ln_gamma", "L0_attn_ln_beta", "L0_attn_in_proj_w", "L0_attn_conv_w", "L0_attn_conv_b",
        "L0_attn_x_proj_w", "L0_attn_dt_proj_w", "L0_attn_dt_proj_b", "L0_attn_A_log", "L0_attn_D",
        "L0_attn_out_proj_w", "L0_ffn_Wg", "L0_ffn_bg", "L0_ffn_W1", "L0_ffn_b1", "L0_ffn_W2", "L0_ffn_b2"]


K_PARTS = [2 * TT, 2 * TT, E, NTOK // P, MAXT, 3, E, E]
K_AT = [sum(K_PARTS[:n]) for n in range(len(K_PARTS) + 1)]
CONSTS = K_AT[-1]


def kernel(**inputs):
    import numpy as np
    import concourse.bacc as bacc
    from concourse.bass_utils import run_bass_kernel_spmd

    nc = bacc.Bacc("TRN2", target_bir_lowering=False, num_devices=1)
    arrays, args = {}, []
    for name in _INS:
        a = np.ascontiguousarray(inputs[name])
        arrays[name] = a
        args.append(nc.dram_tensor(name, a.shape, mybir.dt.from_np(a.dtype), kind="ExternalInput").ap())
    p = np.arange(P)[:, None]
    first_rows = p + P * np.arange(TT).repeat(2)[None] + NTOK * np.tile([0, 1], TT)[None]
    wide = [first_rows - 2 * T, first_rows - T, np.arange(E)[None] * NTOK + 0 * p, np.arange(NTOK // P)[None] * P + 0 * p,
            np.arange(MAXT)[None] + 0 * p, p + P * np.arange(3)[None], np.arange(E)[None] + 0 * p, 1 + 0 * p + np.zeros((1, E))]
    arrays["consts"] = np.concatenate(wide, 1).astype(np.float32)
    c = np.arange(LC)[:, None]
    spare = np.where(c < LC - E, c // (NTOK // P), c - (LC - E) + E)
    arrays["spare_rows"] = (2 * NTOK + P * spare + np.arange(P)[None]).astype(np.float32)
    made = [nc.dram_tensor(n, arrays[n].shape, F32, kind="ExternalInput").ap() for n in ("consts", "spare_rows")]
    spill = nc.dram_tensor("spill", (NTOK, D), F32, kind="Internal").ap()
    row_list = nc.dram_tensor("row_list", (LIST, 1), F32, kind="Internal").ap()
    results = nc.dram_tensor("results", (ROWS, D), F32, kind="Internal").ap()
    out = nc.dram_tensor("out", (B, L, D), F32, kind="ExternalOutput").ap()
    mamba_moe(nc, *made, spill, row_list, results, *args, out)
    r = run_bass_kernel_spmd(nc, [arrays], core_ids=[0])
    return r.results[0]["out"]
```
